# Optimizing a Trainium2 kernel written in Bass

```python
import numpy as np
import jax
import jax.numpy as jnp

def _softmax(x, axis=-1):
    return jax.nn.softmax(x, axis=axis)

def _gelu(x):
    return jax.nn.gelu(x, approximate=True)

def _silu(x):
    return jax.nn.silu(x)

def _sigmoid(x):
    return jax.nn.sigmoid(x)

def _layernorm(x, axis=-1, eps=1e-05):
    m = jnp.mean(x, axis=axis, keepdims=True)
    v = jnp.var(x, axis=axis, keepdims=True)
    return (x - m) / jnp.sqrt(v + eps)

def _scatter_add(tgt, idx, src, axis=0):
    return tgt.at[idx].add(src)

def _segment_sum(src, seg, n):
    return jax.ops.segment_sum(src, seg, n)
kernel_name = 'mk_prb_d1_jaxref_r8_b5fa3d'

def setup_inputs(seed: int=0):
    np.random.seed(seed)
    _w = jnp.asarray

    def _L0_attn_setup():
        import jax, jax.numpy as jnp
        import numpy as np
        import math
        D = 256
        K = 64
        NUM_HEADS = 32
        HEAD_DIM = K // NUM_HEADS
        SPARSITY = 0.1
        LN_EPS = 1e-05
        key = jax.random.key(seed)
        ks = jax.random.split(key, 12)
        B, S = (1, 128)
        sc = 0.02
        inp = {'x': jax.random.normal(ks[0], (B, S, D), dtype=jnp.float32), 'gamma': jnp.ones((D,), jnp.float32), 'beta': jnp.zeros((D,), jnp.float32), 'W1': jax.random.normal(ks[1], (128, D), jnp.float32) * sc, 'b1': jnp.zeros((128,), jnp.float32), 'W2': jax.random.normal(ks[2], (64, 128), jnp.float32) * sc, 'b2': jnp.zeros((64,), jnp.float32), 'W3': jax.random.normal(ks[3], (1, 64), jnp.float32) * sc, 'b3': jnp.zeros((1,), jnp.float32), 'Wqkv': jax.random.normal(ks[4], (3 * K, D), jnp.float32) * sc, 'bqkv': jnp.zeros((3 * K,), jnp.float32), 'Wout': jax.random.normal(ks[5], (D, K), jnp.float32) * sc, 'bout': jnp.zeros((D,), jnp.float32)}
        return inp
    _L0_attn_in = _L0_attn_setup()

    def _L0_ffn_setup():
        import jax, jax.numpy as jnp
        import numpy as np
        B, S, D = (4, 512, 256)
        E, K, I, J = (8, 2, 176, 704)
        CAP_FACTOR = 1.25
        STD = 0.02

        def _moe_routed(x_flat, router, w_up_gate, w_down):
            T, d = x_flat.shape
            logits = jnp.einsum('td,de->te', x_flat, router)
            topk_logits, sel = jax.lax.top_k(logits, K)
            cw = jax.nn.softmax(topk_logits, axis=-1).astype(x_flat.dtype)
            C = int(np.ceil(T * K / E * CAP_FACTOR))
            e_flat = sel.reshape(-1)
            oh = jax.nn.one_hot(e_flat, E, dtype=jnp.int32)
            pos_all = jnp.cumsum(oh, axis=0) - oh
            pos = jnp.take_along_axis(pos_all, e_flat[:, None], axis=1)[:, 0]
            valid = pos < C
            safe_pos = jnp.where(valid, pos, C)
            tok = jnp.repeat(jnp.arange(T), K)
            buf = jnp.zeros((E, C, d), x_flat.dtype).at[e_flat, safe_pos].set(x_flat[tok], mode='drop')
            gate_up = jnp.einsum('ecd,edm->ecm', buf, w_up_gate)
            gate, up = jnp.split(gate_up, [I], axis=-1)
            h = jax.nn.silu(gate) * up
            out_buf = jnp.einsum('eci,eid->ecd', h, w_down)
            gathered = out_buf[e_flat, jnp.minimum(safe_pos, C - 1)]
            gathered = gathered * valid[:, None].astype(x_flat.dtype)
            w = cw.reshape(-1)
            y = jnp.zeros((T, d), x_flat.dtype).at[tok].add(w[:, None] * gathered)
            return y

        def _shared_mlp(x_flat, shared_w_up_gate, shared_w_down):
            gu = jnp.einsum('td,dm->tm', x_flat, shared_w_up_gate)
            gate, up = jnp.split(gu, [J], axis=-1)
            return jnp.einsum('tm,md->td', jax.nn.silu(gate) * up, shared_w_down)
        key = jax.random.key(seed)
        kx, kr, ku, kd, ksu, ksd = jax.random.split(key, 6)
        x = jax.random.normal(kx, (B, S, D), dtype=jnp.float32)
        router = STD * jax.random.truncated_normal(kr, -3, 3, (D, E), dtype=jnp.float32)
        w_up_gate = STD * jax.random.truncated_normal(ku, -3, 3, (E, D, 2 * I), dtype=jnp.float32)
        w_down = STD * jax.random.truncated_normal(kd, -3, 3, (E, I, D), dtype=jnp.float32)
        shared_w_up_gate = STD * jax.random.truncated_normal(ksu, -3, 3, (D, 2 * J), dtype=jnp.float32)
        shared_w_down = STD * jax.random.truncated_normal(ksd, -3, 3, (J, D), dtype=jnp.float32)
        return {'x': x, 'router': router, 'w_up_gate': w_up_gate, 'w_down': w_down, 'shared_w_up_gate': shared_w_up_gate, 'shared_w_down': shared_w_down}
    _L0_ffn_in = _L0_ffn_setup()
    _d = {'L0_attn_x': _L0_attn_in['x'], 'L0_attn_gamma': _L0_attn_in['gamma'], 'L0_attn_beta': _L0_attn_in['beta'], 'L0_attn_W1': _L0_attn_in['W1'], 'L0_attn_b1': _L0_attn_in['b1'], 'L0_attn_W2': _L0_attn_in['W2'], 'L0_attn_b2': _L0_attn_in['b2'], 'L0_attn_W3': _L0_attn_in['W3'], 'L0_attn_b3': _L0_attn_in['b3'], 'L0_attn_Wqkv': _L0_attn_in['Wqkv'], 'L0_attn_bqkv': _L0_attn_in['bqkv'], 'L0_attn_Wout': _L0_attn_in['Wout'], 'L0_attn_bout': _L0_attn_in['bout'], 'L0_ffn_router': _L0_ffn_in['router'], 'L0_ffn_w_up_gate': _L0_ffn_in['w_up_gate'], 'L0_ffn_w_down': _L0_ffn_in['w_down'], 'L0_ffn_shared_w_up_gate': _L0_ffn_in['shared_w_up_gate'], 'L0_ffn_shared_w_down': _L0_ffn_in['shared_w_down']}
    _x0 = _d['L0_attn_x']
    _d['L0_attn_x'] = jax.random.normal(jax.random.fold_in(jax.random.key(seed), 1), (16, 256, 256), dtype=_x0.dtype)
    del _x0
    return _d

def reference(L0_attn_x, L0_attn_gamma, L0_attn_beta, L0_attn_W1, L0_attn_b1, L0_attn_W2, L0_attn_b2, L0_attn_W3, L0_attn_b3, L0_attn_Wqkv, L0_attn_bqkv, L0_attn_Wout, L0_attn_bout, L0_ffn_router, L0_ffn_w_up_gate, L0_ffn_w_down, L0_ffn_shared_w_up_gate, L0_ffn_shared_w_down):

    def _L0_attn_ref(x, gamma, beta, W1, b1, W2, b2, W3, b3, Wqkv, bqkv, Wout, bout):
        import jax, jax.numpy as jnp
        import numpy as np
        import math
        D = 256
        K = 64
        NUM_HEADS = 32
        HEAD_DIM = K // NUM_HEADS
        SPARSITY = 0.1
        LN_EPS = 1e-05
        B, S, d = x.shape
        mu = jnp.mean(x, -1, keepdims=True)
        var = jnp.var(x, -1, keepdims=True)
        xn = (x - mu) * jax.lax.rsqrt(var + LN_EPS) * gamma + beta
        h = jnp.einsum('bsd,fd->bsf', xn, W1)
        pair = jax.nn.relu(h[:, :, None, :] - h[:, None, :, :] + b1)
        pair = jax.nn.relu(jnp.einsum('bijf,gf->bijg', pair, W2) + b2)
        sim = jnp.einsum('bijg,og->bijo', pair, W3)[..., 0] + b3[0]
        diag = jnp.arange(S)
        sim = sim.at[:, diag, diag].set(0.0)
        k_sparse = max(1, int(S * SPARSITY))
        _, top_idx = jax.lax.top_k(sim, k_sparse)
        mask = jnp.full((B, S, S), -jnp.inf, dtype=x.dtype)
        bidx = jnp.arange(B)[:, None, None]
        iidx = jnp.arange(S)[None, :, None]
        mask = mask.at[bidx, iidx, top_idx].set(0.0)
        qkv = jnp.einsum('bsd,ed->bse', xn, Wqkv) + bqkv
        q, k, v = jnp.split(qkv, 3, axis=-1)

        def heads(t):
            return t.reshape(B, S, NUM_HEADS, HEAD_DIM).transpose(0, 2, 1, 3)
        q, k, v = (heads(q), heads(k), heads(v))
        scores = jnp.einsum('bhid,bhjd->bhij', q, k) / math.sqrt(HEAD_DIM)
        scores = scores + mask[:, None, :, :]
        attn = jax.nn.softmax(scores, axis=-1)
        ao = jnp.einsum('bhij,bhjd->bhid', attn, v)
        ao = ao.transpose(0, 2, 1, 3).reshape(B, S, K)
        out = jnp.einsum('bsk,dk->bsd', ao, Wout) + bout
        return x + out

    def _L0_ffn_ref(x, router, w_up_gate, w_down, shared_w_up_gate, shared_w_down):
        import jax, jax.numpy as jnp
        import numpy as np
        B, S, D = (4, 512, 256)
        E, K, I, J = (8, 2, 176, 704)
        CAP_FACTOR = 1.25
        STD = 0.02

        def _moe_routed(x_flat, router, w_up_gate, w_down):
            T, d = x_flat.shape
            logits = jnp.einsum('td,de->te', x_flat, router)
            topk_logits, sel = jax.lax.top_k(logits, K)
            cw = jax.nn.softmax(topk_logits, axis=-1).astype(x_flat.dtype)
            C = int(np.ceil(T * K / E * CAP_FACTOR))
            e_flat = sel.reshape(-1)
            oh = jax.nn.one_hot(e_flat, E, dtype=jnp.int32)
            pos_all = jnp.cumsum(oh, axis=0) - oh
            pos = jnp.take_along_axis(pos_all, e_flat[:, None], axis=1)[:, 0]
            valid = pos < C
            safe_pos = jnp.where(valid, pos, C)
            tok = jnp.repeat(jnp.arange(T), K)
            buf = jnp.zeros((E, C, d), x_flat.dtype).at[e_flat, safe_pos].set(x_flat[tok], mode='drop')
            gate_up = jnp.einsum('ecd,edm->ecm', buf, w_up_gate)
            gate, up = jnp.split(gate_up, [I], axis=-1)
            h = jax.nn.silu(gate) * up
            out_buf = jnp.einsum('eci,eid->ecd', h, w_down)
            gathered = out_buf[e_flat, jnp.minimum(safe_pos, C - 1)]
            gathered = gathered * valid[:, None].astype(x_flat.dtype)
            w = cw.reshape(-1)
            y = jnp.zeros((T, d), x_flat.dtype).at[tok].add(w[:, None] * gathered)
            return y

        def _shared_mlp(x_flat, shared_w_up_gate, shared_w_down):
            gu = jnp.einsum('td,dm->tm', x_flat, shared_w_up_gate)
            gate, up = jnp.split(gu, [J], axis=-1)
            return jnp.einsum('tm,md->td', jax.nn.silu(gate) * up, shared_w_down)
        b, s, d = x.shape
        x_flat = x.reshape(b * s, d)
        routed = _moe_routed(x_flat, router, w_up_gate, w_down)
        shared = _shared_mlp(x_flat, shared_w_up_gate, shared_w_down)
        return (routed + shared).reshape(b, s, d)
    x = L0_attn_x
    xn = _layernorm(x, axis=-1)
    x = x + _L0_attn_ref(xn, L0_attn_gamma, L0_attn_beta, L0_attn_W1, L0_attn_b1, L0_attn_W2, L0_attn_b2, L0_attn_W3, L0_attn_b3, L0_attn_Wqkv, L0_attn_bqkv, L0_attn_Wout, L0_attn_bout) + _L0_ffn_ref(xn, L0_ffn_router, L0_ffn_w_up_gate, L0_ffn_w_down, L0_ffn_shared_w_up_gate, L0_ffn_shared_w_down)
    return x

_drawn_inputs = setup_inputs


def setup_inputs(seed=0):
    import zlib

    import numpy as np

    out = dict(_drawn_inputs(seed))
    spreads = {'L0_attn_gamma': (1.0, 0.6),
     'L0_attn_beta': (0.0, 0.8),
     'L0_attn_b1': (0.0, 0.8),
     'L0_attn_b2': (0.0, 0.8),
     'L0_attn_bqkv': (0.0, 0.8),
     'L0_attn_bout': (0.0, 0.734)}
    factors = {'L0_attn_W1': 8.0,
     'L0_attn_W2': 8.0,
     'L0_attn_W3': 8.0,
     'L0_attn_Wqkv': 8.0,
     'L0_attn_Wout': 5.594,
     'L0_ffn_router': 8.0,
     'L0_ffn_w_up_gate': 8.0,
     'L0_ffn_w_down': 8.0,
     'L0_ffn_shared_w_up_gate': 4.22,
     'L0_ffn_shared_w_down': 4.214}
    for name, (base, spread) in spreads.items():
        noise = np.random.default_rng([zlib.crc32(name.encode()), seed]).standard_normal(out[name].shape)
        drawn = base * np.exp(spread * noise) if base else spread * noise
        out[name] = jnp.asarray(drawn.astype(out[name].dtype))
    for name, factor in factors.items():
        out[name] = (out[name] * factor).astype(out[name].dtype)
    return out
```

```python
import concourse.bass as bass
from concourse import mybir
from contextlib import ExitStack


def lsn_attention_moe_block(
    nc: bass.Bass,
    x_d: bass.AP,
    gamma_d: bass.AP,
    beta_d: bass.AP,
    w1t_d: bass.AP,
    b1_d: bass.AP,
    w2t_d: bass.AP,
    b2_d: bass.AP,
    w3_d: bass.AP,
    b3_d: bass.AP,
    wqkvt_d: bass.AP,
    bqkv_d: bass.AP,
    woutt_d: bass.AP,
    bout_d: bass.AP,
    router_d: bass.AP,
    wug_d: bass.AP,
    wdn_d: bass.AP,
    swug_d: bass.AP,
    swdn_d: bass.AP,
    out_d: bass.AP,
):
    f32 = mybir.dt.float32
    u32 = mybir.dt.uint32
    ALU = mybir.AluOpType
    ACT = mybir.ActivationFunctionType
    AX = mybir.AxisListType.X
    ds = bass.ds

    P = 128
    NB, S, D = x_d.shape
    DC = D // P
    NT = NB * S // P
    HALVES = S // P
    F1, G2 = w2t_d.shape
    KD = woutt_d.shape[0]
    HEADS, HD = 32, KD // 32
    TOPK = max(1, int(S * 0.1))
    ROUNDS = (TOPK + 7) // 8
    EPS = 1e-5
    SCALE = float(HD) ** -0.5
    E = router_d.shape[1]
    TOKENS = NB * S
    CAP = -(-TOKENS * 2 * 5 // (E * 4))
    SLOTS = E * CAP
    I = wdn_d.shape[1]
    IM = I // 2
    J = swdn_d.shape[0]
    JC = (J + P - 1) // P
    LOWEST = -3.0e38

    UNIT = 4
    STEP_ROWS = 2 * UNIT
    STEPS = P // STEP_ROWS
    BSTEPS = HALVES * STEPS
    R1 = 4
    R2 = 4

    NPE = CAP // P
    GPE = NPE // 2
    GB = 2 * GPE
    CT = 4
    NCH = NT // CT

    x_t = x_d.rearrange("b (h p) d -> p (b h) d", p=P)
    out_t = out_d.rearrange("b (h p) d -> p (b h) d", p=P)
    kv_dram = nc.dram_tensor("kv_rows", (TOKENS, 2 * KD), f32, kind="Internal").ap()
    slot_dram = nc.dram_tensor("slot_inputs", (SLOTS, D), f32, kind="Internal").ap()
    yslot_dram = nc.dram_tensor("slot_outputs", (SLOTS, D), f32, kind="Internal").ap()

    ctx = ExitStack()
    with ctx:
        def sb(name, shape, dt=f32):
            return ctx.enter_context(nc.sbuf_tensor(name, shape, dt))

        def sem(name):
            return ctx.enter_context(nc.semaphore(name))

        xn1 = sb("xn1", [P, NT, D])
        xT1 = sb("xT1", [P, DC, TOKENS])
        qao = sb("qao", [P, NT, KD])
        w1t = sb("w1t", [P, DC, F1])
        wqkvt = sb("wqkvt", [P, DC, 3 * KD])
        router = sb("router", [P, DC, E])
        w2t = sb("w2t", [F1, G2])
        w3win = sb("w3win", [2 * G2, 64])
        woutt = sb("woutt", [KD, D])
        gamma = sb("gamma", [P, DC])
        beta = sb("beta", [P, DC])
        b1 = sb("b1", [F1, 1])
        b2 = sb("b2", [2 * G2, 1])
        b3 = sb("b3", [P, 1])
        bqkv = sb("bqkv", [P, 3 * KD])
        bout = sb("bout", [P, D])
        ident = sb("ident", [P, P])
        earlier = sb("earlier", [P, P])
        ones = sb("ones", [P, P])
        iota8 = sb("iota8", [P, E])
        batch_row = sb("batch_row", [P, NB])
        route_w = sb("route_w", [P, NT, 2])
        slot_get = sb("slot_get", [P, NT, 2], u32)
        slot_put = sb("slot_put", [P, NT * 2], u32)

        ARENA = 31700
        arena = sb("arena", [P, ARENA])
        taken = [0]

        def part(n, *dims):
            at = taken[0]
            taken[0] = at + n
            assert taken[0] <= ARENA
            view = arena[:, at:at + n]
            if len(dims) == 1:
                return view.rearrange("p (a b) -> p a b", a=dims[0])
            if len(dims) == 2:
                return view.rearrange("p (a b c) -> p a b c", a=dims[0], b=dims[1])
            return view

        hneg = part(TOKENS)
        hb = part(TOKENS)
        pair_base = taken[0]
        r1 = part(R1 * STEP_ROWS * S, R1, STEP_ROWS)
        r2 = part(R2 * 2 * 512, R2)
        kvg = part(2 * TOPK * 2 * KD, 2, TOPK)
        prod = part(TOPK * KD, TOPK)
        sc = part(TOPK * HEADS, TOPK)
        pv = part(TOPK * KD, TOPK)
        z0 = part(S)
        z1 = part(S)
        z2 = part(S)
        pair_end = taken[0]
        top8 = sb("top8", [P, ROUNDS, 8])
        idx8 = sb("idx8", [P, ROUNDS, 8], u32)
        gidx = sb("gidx", [P, 2, ROUNDS * 8], u32)
        smax = sb("smax", [P, HEADS])
        sden = sb("sden", [P, HEADS])
        srec = sb("srec", [P, HEADS])
        aosum = sb("aosum", [P, KD])

        taken[0] = pair_base
        xn1s = part(HALVES * D, HALVES)
        xn2s = part(HALVES * D, HALVES)
        xT1s = part(DC * S, DC)
        xn2T = part(DC * S, DC)
        kvs = part(HALVES * 2 * KD, HALVES)
        stats = part(2 * HALVES * 6, 2, HALVES)
        mv = part(2 * HALVES * 2, 2, HALVES)
        veps = part(2 * HALVES, 2)
        rstd = part(2 * HALVES, 2)
        neg_half = part(HALVES)
        logits = part(NT * E, NT)
        zeros = part(SLOTS // P * D // 5)
        best = part(NT * E, NT)
        besti = sb("besti", [P, NT, E], u32)
        expert = part(NT * 2, NT)
        dlog = part(NT)
        edlog = part(NT)
        eden = part(NT)
        hot = [part(NT * E, NT) for _ in range(2)]
        hots = part(NT * E, NT)
        filled = part(NT * E, NT)
        base = part(NT * E, NT)
        hotpos = [part(NT * E, NT) for _ in range(2)]
        pos = part(NT * 2, NT)
        posc = part(NT * 2, NT)
        slotf = part(NT * 2, NT)
        over = part(NT * 2, NT)
        valid = part(NT * 2, NT)
        assert taken[0] <= pair_end

        taken[0] = 0
        xe = [part(NPE * D, NPE) for _ in range(2)]
        wug = [part(DC * 2 * I, DC) for _ in range(2)]
        wdn = [part(2 * D, 2) for _ in range(2)]
        xTe = [part(DC * 256, DC) for _ in range(2)]
        sge = [part(2 * 256, 2) for _ in range(2)]
        hTe = [part(2 * 256, 2) for _ in range(2)]
        oute = [part(NPE * D, NPE) for _ in range(2)]
        swug = part(DC * 2 * J, DC)
        swdn = part(JC * D, JC)
        sgs = [part(512) for _ in range(2)]
        hTs = part(JC * 512, JC)
        aos = part(CT * KD, CT)
        aoT = part(512)
        ys = part(CT * 2 * D, CT, 2)
        resid = part(CT * D, CT)
        fin = part(CT * D, CT)
        ysidx = sb("ysidx", [P, CT, 2], u32)

        ps = ctx.enter_context(nc.psum_tensor("ps", [P, 8, 512], f32))

        ps_t1 = ps[:, 0, :].rearrange("p (c s) -> p c s", c=DC)
        ps_t2 = ps[:, 1, :].rearrange("p (c s) -> p c s", c=DC)
        ps_h = ps[:, 2, 0:S]
        ps_qkv = ps[:, 3, :].rearrange("p (h n) -> p h n", h=HALVES)
        ps_logit = ps[:, 4, 0:HALVES * E].rearrange("p (h n) -> p h n", h=HALVES)
        ps_before = ps[:, 5, 0:NT * E].rearrange("p (t e) -> p t e", e=E)
        ps_count = ps[:, 6, 0:NT * E].rearrange("p (t e) -> p t e", e=E)

        def ps_l2(g):
            return ps[:, 2 * (g % 2):2 * (g % 2) + 2, :]

        def ps_sim(h):
            return ps[:, 4 + h, 0:S]

        def ps_xt(g):
            return ps[:, 6 + g % 2, :].rearrange("p (c n) -> p c n", c=DC)

        def ps_gate(g):
            return ps[0:IM, 2 * (g % 2), :].rearrange("p (m n) -> p m n", m=2)

        def ps_up(g):
            return ps[0:IM, 2 * (g % 2) + 1, :].rearrange("p (m n) -> p m n", m=2)

        def ps_down(g):
            return ps[:, 4 + g % 2, :].rearrange("p (n d) -> p n d", n=2)

        consts_loaded = sem("consts_loaded")
        x_first_loaded = sem("x_first_loaded")
        x_rest_loaded = sem("x_rest_loaded")
        made = sem("made")
        ln_step = sem("ln_step")
        rstd_ready = sem("rstd_ready")
        t1_ready = sem("t1_ready")
        t2_ready = sem("t2_ready")
        xT1s_ready = sem("xT1s_ready")
        xn2T_ready = sem("xn2T_ready")
        h_ready = sem("h_ready")
        h_saved = sem("h_saved")
        qkv_ready = sem("qkv_ready")
        qkv_saved = sem("qkv_saved")
        kv_stored = sem("kv_stored")
        xn1_kept = sem("xn1_kept")
        xT1_kept = sem("xT1_kept")
        slots_zeroed = sem("slots_zeroed")
        route_step = sem("route_step")
        hot_ready = sem("hot_ready")
        dlog_ready = sem("dlog_ready")
        exp_routed = sem("exp_routed")
        counts_ready = sem("counts_ready")
        route_done = sem("route_done")
        scattered = sem("scattered")

        r1_dve = sem("r1_dve")
        r1_act = sem("r1_act")
        l2_done = sem("l2_done")
        r2_done = sem("r2_done")
        l3_done = sem("l3_done")
        sim_copied = sem("sim_copied")
        diag_cleared = sem("diag_cleared")
        topk_step = sem("topk_step")
        idx_ready = sem("idx_ready")
        gathered = sem("gathered")
        prod_ready = sem("prod_ready")
        attn_step = sem("attn_step")
        exp_ready = sem("exp_ready")

        xe_loaded = [sem(f"xe_loaded{i}") for i in range(2)]
        we_loaded = [sem(f"we_loaded{i}") for i in range(2)]
        xt_done = sem("xt_done")
        xt_copied = sem("xt_copied")
        gu_done = sem("gu_done")
        silu_done = sem("silu_done")
        mul_done = sem("mul_done")
        down_done = sem("down_done")
        down_copied = sem("down_copied")
        y_stored = [sem(f"y_stored{i}") for i in range(2)]

        shared_loaded = sem("shared_loaded")
        sgu_done = sem("sgu_done")
        ssilu_done = sem("ssilu_done")
        smul_done = sem("smul_done")
        ao_fetched = sem("ao_fetched")
        aoT_done = sem("aoT_done")
        aoT_copied = sem("aoT_copied")
        sdown_done = sem("sdown_done")
        ysidx_ready = sem("ysidx_ready")
        ys_gathered = sem("ys_gathered")
        resid_loaded = sem("resid_loaded")
        resid_ready = sem("resid_ready")
        comb_step = sem("comb_step")
        out_stored = sem("out_stored")

        START = 1
        started = [ln_step, t1_ready, t2_ready, xT1s_ready, xn2T_ready, h_saved, qkv_ready, qkv_saved, kv_stored, xn1_kept,
                   xT1_kept, down_copied, y_stored[0], y_stored[1], comb_step, aoT_done, aoT_copied, sdown_done, out_stored]

        N_CONST = 13 + 2 * DC
        CONSTS = 16 * N_CONST
        LN = 2 * (3 * HALVES + 1)
        TS = 4 * ROUNDS - 1
        AS = 8
        CS = 3 * CT

        GROUPS = STEPS // 2

        def dve_rows(s):
            return 6 if s % STEPS in (2, 8, 9, 15) else 5

        passed = {name: sem(f"{name}_passed") for name in ("dve", "pe", "pool")}

        def wait_alone(eng, name, what, value):
            eng.wait_ge(what, value)
            eng.sem_inc(passed[name], 1)

        block = ctx.enter_context(nc.Block())

        @block.sync
        def _(sp):
            sp.dma_start(xn1[:, 0:HALVES, :], x_t[:, 0:HALVES, :]).then_inc(x_first_loaded, 16)
            for s in started:
                sp.sem_inc(s, START)
            for dst, src in (
                (w1t[:, :, :], w1t_d.rearrange("(c p) f -> p c f", p=P)),
                (wqkvt[:, :, :], wqkvt_d.rearrange("(c p) f -> p c f", p=P)),
                (router[:, :, :], router_d.rearrange("(c p) f -> p c f", p=P)),
                *((to[:, c:c + 1], src[c * P:(c + 1) * P].rearrange("(p o) -> p o", o=1))
                  for to, src in ((gamma, gamma_d), (beta, beta_d)) for c in range(DC)),
                (b1[:, :], b1_d.rearrange("(p o) -> p o", o=1)),
                (bqkv[:, :], bqkv_d.partition_broadcast(P)),
                (w2t[:, :], w2t_d),
                (b2[0:G2, :], b2_d.rearrange("(p o) -> p o", o=1)),
                (b2[G2:2 * G2, :], b2_d.rearrange("(p o) -> p o", o=1)),
                (b3[:, :], b3_d.partition_broadcast(P)),
                (woutt[:, :], woutt_d),
                (bout[:, :], bout_d.partition_broadcast(P)),
            ):
                sp.dma_start(dst, src).then_inc(consts_loaded, 16)
            sp.wait_ge(made, 1)
            sp.dma_start(w3win[0:G2, 32:33], w3_d.rearrange("o g -> g o")).then_inc(consts_loaded, 16)
            sp.dma_start(w3win[G2:2 * G2, 34:35], w3_d.rearrange("o g -> g o")).then_inc(consts_loaded, 16)
            rest = NT - HALVES
            for i in range(3):
                a, b = HALVES + rest * i // 3, HALVES + rest * (i + 1) // 3
                sp.dma_start(xn1[:, a:b, :], x_t[:, a:b, :]).then_inc(x_rest_loaded, 16)
            sp.wait_ge(made, 2)
            zv = slot_dram.rearrange("(k p n) d -> k p (n d)", k=5, p=P)
            for k in range(5):
                sp.dma_start(zv[k], zeros).then_inc(slots_zeroed, 16)
            with sp.Fori(0, NB) as b:
                sp.wait_ge(qkv_saved, START + b * 3 + 3)
                sp.dma_start(kv_dram[ds(b * S, S), :].rearrange("(h p) n -> p h n", p=P), kvs)\
                  .then_inc(kv_stored, 16)

            sp.wait_ge(attn_step, AS * NT)
            sp.wait_ge(scattered, 16 * 2 * NT)

            def load_expert(e, i):
                sp.dma_start(xe[i], slot_dram[ds(e * CAP, CAP), :].rearrange("(p n) d -> p n d", p=P))\
                  .then_inc(xe_loaded[i], 16)
                sp.dma_start(wug[i], wug_d[ds(e, 1), :, :].rearrange("o (c p) m -> p (o c) m", p=P))\
                  .then_inc(we_loaded[i], 16)
                sp.dma_start(wdn[i][0:IM], wdn_d[ds(e, 1), :, :].rearrange("o (m p) d -> p (o m) d", p=IM))\
                  .then_inc(we_loaded[i], 16)

            def store_expert(e, i, last_group):
                sp.wait_ge(down_copied, START + last_group)
                sp.dma_start(yslot_dram[ds(e * CAP, CAP), :].rearrange("(p n) d -> p n d", p=P), oute[i])\
                  .then_inc(y_stored[i], 16)

            for i in range(2):
                load_expert(i, i)
            sp.dma_start(swug, swug_d.rearrange("(c p) m -> p c m", p=P)).then_inc(shared_loaded, 16)
            full = J // P
            sp.dma_start(swdn[:, 0:full, :], swdn_d[0:full * P, :].rearrange("(c p) d -> p c d", p=P))\
              .then_inc(shared_loaded, 16)
            sp.dma_start(swdn[0:J - full * P, full, :], swdn_d[full * P:J, :]).then_inc(shared_loaded, 16)
            with sp.Fori(0, E // 2 - 1) as j:
                for i in range(2):
                    sp.wait_ge(down_done, j * GB + GPE * (i + 1))
                    load_expert(j * 2 + (2 + i), i)
                    store_expert(j * 2 + i, i, j * GB + GPE * (i + 1))
            for i in range(2):
                store_expert(E - 2 + i, i, GB * (E // 2 - 1) + GPE * (i + 1))

            def load_resid(c):
                sp.wait_ge(comb_step, START + c * CS)
                sp.dma_start(resid, x_t[:, ds(c * CT, CT), :]).then_inc(resid_loaded, 16)

            load_resid(0)
            with sp.Fori(0, NCH - 1) as c:
                load_resid(c + 1)
                sp.dma_start(out_t[:, ds(c * CT, CT), :], fin).then_inc(out_stored, 16)
            sp.wait_ge(comb_step, START + NCH * CS)
            sp.dma_start(out_t[:, (NCH - 1) * CT:NCH * CT, :], fin).then_inc(out_stored, 16)
            sp.wait_ge(out_stored, START + 16 * NCH)

        @block.gpsimd
        def _(pool):
            nc.gpsimd.memset(w3win[:, :], 0.0).then_inc(made, 1)
            nc.gpsimd.memset(zeros, 0.0).then_inc(made, 1)
            nc.gpsimd.memset(ident[:, :], 0.0).then_inc(made, 1)
            nc.gpsimd.memset(earlier[:, :], 1.0).then_inc(made, 1)
            nc.gpsimd.memset(ones[:, :], 1.0).then_inc(made, 1)
            nc.gpsimd.memset(neg_half, -0.5).then_inc(made, 1)
            pool.wait_ge(made, 6)
            nc.gpsimd.affine_select(out=ident[:, :], in_=ident[:, :], compare_op=ALU.not_equal, fill=1.0, base=0,
                                    pattern=[[-1, P]], channel_multiplier=1).then_inc(made, 1)
            nc.gpsimd.affine_select(out=earlier[:, :], in_=earlier[:, :], compare_op=ALU.is_gt, fill=0.0, base=0,
                                    pattern=[[1, P]], channel_multiplier=-1).then_inc(made, 1)
            nc.gpsimd.iota(iota8[:, :], pattern=[[1, E]], base=0, channel_multiplier=0,
                           allow_small_or_imprecise_dtypes=True).then_inc(made, 1)
            nc.gpsimd.iota(batch_row[:, :], pattern=[[S, NB]], base=0, channel_multiplier=0,
                           allow_small_or_imprecise_dtypes=True).then_inc(made, 1)

            with pool.Fori(0, NB) as b:
                for r in range(2):
                    pool.wait_ge(ln_step, START + b * LN + (r * (LN // 2) + 2 * HALVES + 1))
                    nc.gpsimd.tensor_tensor(rstd[:, r, :], veps[:, r, :], neg_half, ALU.pow).then_inc(rstd_ready, 1)
                pool.wait_ge(ln_step, START + b * LN + LN // 2)
                nc.gpsimd.tensor_copy(xn1[:, ds(b * HALVES, HALVES), :], xn1s).then_inc(xn1_kept, 1)
                pool.wait_ge(xT1s_ready, START + b + 1)
                nc.gpsimd.tensor_copy(xT1[:, :, ds(b * S, S)], xT1s).then_inc(xT1_kept, 1)

            pool.wait_ge(xn1_kept, START + NB)
            pool.wait_ge(slots_zeroed, 16 * 5)
            pool.wait_ge(route_done, 1)
            for t in range(NT):
                for k in range(2):
                    pool.indirect_dma_start(
                        out=slot_dram, out_offset=bass.IndirectOffsetOnAxis(ap=slot_put[:, 2 * t + k:2 * t + k + 1], axis=0),
                        in_=xn1[:, t, :], in_offset=None, bounds_check=SLOTS - 1, oob_is_err=False).then_inc(scattered, 16)

            pool.wait_ge(kv_stored, START + 16 * NB)

            def gather_tile(t, h, first):
                wait_alone(pool, "pool", sim_copied, t + 1)
                nc.gpsimd.affine_select(out=z0, in_=z0, compare_op=ALU.not_equal, fill=0.0, base=P * h,
                                        pattern=[[-1, S]], channel_multiplier=1).then_inc(diag_cleared, 1)
                if not first:
                    wait_alone(pool, "pool", attn_step, (t - 1) * AS)
                for r in range(TOPK):
                    if r % 8 == 0:
                        wait_alone(pool, "pool", idx_ready, t * ROUNDS + (r // 8 + 1))
                    pool.indirect_dma_start(
                        out=kvg[:, h, r, :], out_offset=None, in_=kv_dram,
                        in_offset=bass.IndirectOffsetOnAxis(ap=gidx[:, h, r:r + 1], axis=0)).then_inc(gathered, 16)
                pool.wait_ge(gathered, (t + 1) * (16 * TOPK))
                pool.wait_ge(attn_step, (t - 1) * AS + 1) if not first else None
                nc.gpsimd.tensor_tensor(prod, kvg[:, h, :, 0:KD],
                                        qao[:, ds(t, 1), :].to_broadcast([P, TOPK, KD]), ALU.mult)\
                    .then_inc(prod_ready, 1)

            gather_tile(0, 0, True)
            gather_tile(1, 1, False)
            with pool.Fori(1, NB) as b:
                gather_tile(b * HALVES, 0, False)
                gather_tile(b * HALVES + 1, 1, False)

            pool.wait_ge(y_stored[0], START + 16 * (E // 2))
            pool.wait_ge(y_stored[1], START + 16 * (E // 2))
            with pool.Fori(0, NCH) as c:
                pool.wait_ge(comb_step, START + c * CS)
                pool.wait_ge(aoT_done, START + c)
                nc.gpsimd.tensor_copy(aos, qao[:, ds(c * CT, CT), :]).then_inc(ao_fetched, 1)
                nc.gpsimd.tensor_copy(ysidx[:, :, :], slot_get[:, ds(c * CT, CT), :]).then_inc(ysidx_ready, 1)
                wait_alone(pool, "pool", ysidx_ready, c + 1)
                for n in range(CT):
                    for k in range(2):
                        pool.indirect_dma_start(
                            out=ys[:, n, k, :], out_offset=None, in_=yslot_dram,
                            in_offset=bass.IndirectOffsetOnAxis(ap=ysidx[:, n, k:k + 1], axis=0)).then_inc(ys_gathered, 16)
                pool.wait_ge(resid_loaded, c * 16 + 16)
                nc.gpsimd.tensor_tensor(resid, resid, xn1[:, ds(c * CT, CT), :], ALU.add).then_inc(resid_ready, 1)
                pool.wait_ge(resid_ready, c * 2 + 1)
                nc.gpsimd.tensor_tensor(resid, resid, bout[:, :].unsqueeze(1).to_broadcast([P, CT, D]), ALU.add)\
                    .then_inc(resid_ready, 1)

        @block.tensor
        def _(pe):
            pe.wait_ge(consts_loaded, CONSTS)
            pe.wait_ge(made, 10)
            with pe.Fori(0, NB) as b:
                pe.wait_ge(ln_step, START + b * LN + LN // 2)
                pe.wait_ge(xT1s_ready, START + b)
                for h in range(HALVES):
                    for c in range(DC):
                        last = nc.tensor.transpose(ps_t1[:, c, h * P:(h + 1) * P], xn1s[:, h, c * P:(c + 1) * P], ident[:, :])
                last.then_inc(t1_ready, 1)
                pe.wait_ge(ln_step, START + b * LN + LN)
                pe.wait_ge(xn2T_ready, START + b * DC)
                for h in range(HALVES):
                    for c in range(DC):
                        last = nc.tensor.transpose(ps_t2[:, c, h * P:(h + 1) * P], xn2s[:, h, c * P:(c + 1) * P], ident[:, :])
                last.then_inc(t2_ready, 1)
                pe.wait_ge(xT1s_ready, START + b + 1)
                pe.wait_ge(qkv_saved, START + b * 3)
                for h in range(HALVES):
                    for c in range(DC):
                        nc.tensor.matmul(ps_logit[:, h, :], xT1s[:, c, h * P:(h + 1) * P], router[:, c, :],
                                         start=(c == 0), stop=(c == DC - 1))
                pe.wait_ge(xn2T_ready, START + b * DC + DC)
                pe.wait_ge(h_saved, START + b * 2)
                for c in range(DC):
                    last = nc.tensor.matmul(ps_h, w1t[:, c, :], xn2T[:, c, :], start=(c == 0), stop=(c == DC - 1))
                last.then_inc(h_ready, 1)
                for h in range(HALVES):
                    for c in range(DC):
                        last = nc.tensor.matmul(ps_qkv[:, h, 0:3 * KD], xn2T[:, c, h * P:(h + 1) * P], wqkvt[:, c, :],
                                                start=(c == 0), stop=(c == DC - 1))
                last.then_inc(qkv_ready, 1)

            pe.wait_ge(hot_ready, 1)
            pe.wait_ge(h_saved, START + 2 * NB)
            hv = hots.rearrange("p t e -> p (t e)")
            nc.tensor.matmul(ps_before.rearrange("p t e -> p (t e)"), earlier[:, :], hv, start=True, stop=True)
            nc.tensor.matmul(ps_count.rearrange("p t e -> p (t e)"), ones[:, :], hv, start=True, stop=True)\
                .then_inc(counts_ready, 1)


            pe.wait_ge(route_done, 1)

            def layer2(b, s, first):
                pe.wait_ge(r1_dve, b * BSTEPS + (s + 1))
                pe.wait_ge(r1_act, b * BSTEPS + (s + 1))
                if not (first and s < 2):
                    pe.wait_ge(r2_done, b * BSTEPS + (s - 1))
                for u in range(2):
                    for v in range(2):
                        last = nc.tensor.matmul(ps_l2(s)[v * G2:(v + 1) * G2, u, :], w2t[:, :],
                                                r1[:, s % R1, 4 * u + 2 * v:4 * u + 2 * v + 2, :], start=True, stop=True)
                last.then_inc(l2_done, 1)

            def layer3(steps, s):
                pe.wait_ge(r2_done, steps)
                q, h = s % STEPS // 2, s // STEPS
                for a in range(2):
                    for c in range(4):
                        at = 32 - (UNIT * q + a)
                        last = nc.tensor.matmul(ps_sim(h)[32 * c:32 * c + 32, :], w3win[:, at:at + 32],
                                                r2[:, (s - 1 + c // 2) % R2, 512 * (c % 2) + a * S:512 * (c % 2) + (a + 1) * S],
                                                start=(q == 0 and a == 0), stop=(q == GROUPS - 1 and a == 1))
                last.then_inc(l3_done, 1)

            def pair_batch(b, first):
                for s in range(BSTEPS):
                    layer2(b, s, first)
                    if s == 0 and not first:
                        layer3(b * BSTEPS, BSTEPS - 1)
                    elif s % 2 == 0 and s:
                        if s % STEPS == 2 and not first:
                            pe.wait_ge(sim_copied, b * HALVES + (s // STEPS - 1))
                        layer3(b * BSTEPS + s, s - 1)

            pair_batch(0, True)
            with pe.Fori(1, NB) as b:
                pair_batch(b, False)
            layer3(NB * BSTEPS, BSTEPS - 1)

            pe.wait_ge(sim_copied, NT)

            def transpose_slots(j, g):
                if g >= 2:
                    pe.wait_ge(xt_copied, j * GB + (g - 1))
                i, n0 = g // GPE, 2 * (g % GPE)
                if g % GPE == 0:
                    pe.wait_ge(xe_loaded[i], j * 16 + 16)
                for n in range(2):
                    for c in range(DC):
                        last = nc.tensor.transpose(ps_xt(g)[:, c, n * P:(n + 1) * P],
                                                   xe[i][:, n0 + n, c * P:(c + 1) * P], ident[:, :])
                last.then_inc(xt_done, 1)

            def gate_up(j, g):
                i = g // GPE
                if g % GPE == 0:
                    pe.wait_ge(we_loaded[i], j * 32 + 32)
                pe.wait_ge(xt_copied, j * GB + (g + 1))
                if g >= 2:
                    pe.wait_ge(mul_done, j * GB + (g - 1))
                for to, col in ((ps_gate(g), 0), (ps_up(g), I)):
                    for m in range(2):
                        for c in range(DC):
                            last = nc.tensor.matmul(to[:, m, :], wug[i][:, c, col + m * IM:col + (m + 1) * IM],
                                                    xTe[g % 2][:, c, :], start=(c == 0), stop=(c == DC - 1))
                last.then_inc(gu_done, 1)

            def down(j, g):
                pe.wait_ge(mul_done, j * GB + (g + 1))
                if g >= 2:
                    pe.wait_ge(down_copied, START + j * GB + (g - 1))
                for n in range(2):
                    for m in range(2):
                        last = nc.tensor.matmul(ps_down(g)[:, n, :], hTe[g % 2][0:IM, m, n * P:(n + 1) * P],
                                                wdn[g // GPE][0:IM, m, :], start=(m == 0), stop=(m == 1))
                last.then_inc(down_done, 1)

            with pe.Fori(0, E // 2) as j:
                pe.wait_ge(down_copied, START + j * GB)
                transpose_slots(j, 0)
                for g in range(GB):
                    if g < GB - 1:
                        transpose_slots(j, g + 1)
                    gate_up(j, g)
                    if g:
                        down(j, g - 1)
                down(j, GB - 1)

            pe.wait_ge(shared_loaded, 16 * 3)
            pe.wait_ge(down_copied, START + GB * (E // 2))
            with pe.Fori(0, NCH) as c:
                for m in range(JC):
                    w = min(P, J - m * P)
                    if m >= 2:
                        wait_alone(pe, "pe", smul_done, c * JC + (m - 1))
                    for up in range(2):
                        for k in range(DC):
                            last = nc.tensor.matmul(ps[0:w, 2 * (m % 2) + up, :], swug[:, k, up * J + m * P:up * J + m * P + w],
                                                    xT1[:, k, ds(c * (CT * P), CT * P)], start=(k == 0), stop=(k == DC - 1))
                    last.then_inc(sgu_done, 1)
                pe.wait_ge(ao_fetched, c + 1)
                wait_alone(pe, "pe", aoT_copied, START + c)
                for n in range(CT):
                    last = nc.tensor.transpose(ps[0:KD, 4, n * P:(n + 1) * P], aos[:, n, :], ident[:, :])
                last.then_inc(aoT_done, 1)
                pe.wait_ge(smul_done, c * JC + JC)
                pe.wait_ge(aoT_copied, START + c + 1)
                pe.wait_ge(comb_step, START + c * CS)
                for n in range(CT):
                    to = ps[:, 6 + n // 2, (n % 2) * D:(n % 2 + 1) * D]
                    for m in range(JC):
                        w = min(P, J - m * P)
                        nc.tensor.matmul(to, hTs[0:w, m, n * P:(n + 1) * P], swdn[0:w, m, :], start=(m == 0), stop=False)
                    nc.tensor.matmul(to, aoT[0:KD, n * P:(n + 1) * P], woutt[:, :], start=False, stop=True)\
                        .then_inc(sdown_done, 1)

        def step_rows(s):
            return [32 * (2 * (s % 2) + k // UNIT) + UNIT * (s % STEPS // 2) + k % UNIT for k in range(STEP_ROWS)]

        @block.scalar
        def _(act):
            act.wait_ge(consts_loaded, CONSTS)
            with act.Fori(0, NB) as b:
                act.wait_ge(t1_ready, START + b + 1)
                act.wait_ge(qkv_ready, START + b)
                act.wait_ge(xT1_kept, START + b)
                nc.scalar.activation(xT1s, ps_t1, ACT.Copy).then_inc(xT1s_ready, 1)
                act.wait_ge(t2_ready, START + b + 1)
                for c in range(DC):
                    nc.scalar.activation(xn2T[:, c, :], ps_t2[:, c, :], ACT.Identity, scale=gamma[:, c:c + 1],
                                         bias=beta[:, c:c + 1]).then_inc(xn2T_ready, 1)
                act.wait_ge(h_ready, b + 1)
                nc.scalar.activation(hneg[:, ds(b * S, S)], ps_h, ACT.Copy, scale=-1.0).then_inc(h_saved, 1)
                nc.scalar.activation(hb[:, ds(b * S, S)], ps_h, ACT.Identity, bias=b1[:, 0:1]).then_inc(h_saved, 1)
            act.wait_ge(dlog_ready, 1)
            nc.scalar.activation(edlog, dlog, ACT.Exp).then_inc(exp_routed, 1)

            act.wait_ge(route_done, 1)
            act.wait_ge(slots_zeroed, 16 * 5)
            act.wait_ge(kv_stored, START + 16 * NB)
            act.wait_ge(h_saved, START + 2 * NB)
            act.wait_ge(xn1_kept, START + NB)
            act.wait_ge(xT1_kept, START + NB)

            def relu1(b, s, first):
                if not (first and s < R1):
                    act.wait_ge(l2_done, b * BSTEPS + (s - R1 + 1))
                rows = step_rows(s)
                for k in range(dve_rows(s), STEP_ROWS):
                    at = b * S + ((s // STEPS) * P + rows[k])
                    last = nc.scalar.activation(r1[:, s % R1, k, :], hneg[:, ds(b * S, S)], ACT.Relu, bias=hb[:, ds(at, 1)])
                last.then_inc(r1_act, 1)

            def relu2(steps, s, wait_group):
                act.wait_ge(l2_done, steps)
                if wait_group is not None:
                    act.wait_ge(l3_done, wait_group)
                nc.scalar.activation(r2[:, s % R2, :].rearrange("p (u n) -> p u n", u=2), ps_l2(s), ACT.Relu, bias=b2[:, 0:1]).then_inc(r2_done, 1)

            def copy_sim(t, h, first):
                act.wait_ge(l3_done, t * GROUPS + GROUPS)
                if not first:
                    act.wait_ge(topk_step, t * TS + (3 - TS))
                nc.scalar.activation(z0, ps_sim(h), ACT.Identity, bias=b3[:, 0:1]).then_inc(sim_copied, 1)

            def exp_scores(t):
                act.wait_ge(attn_step, t * AS + 3)
                nc.scalar.activation(sc, sc, ACT.Exp, scale=SCALE).then_inc(exp_ready, 1)

            def pair_batch(b, first):
                for s in range(BSTEPS):
                    h = s // STEPS
                    relu1(b, s, first)
                    if not (first and s == 0):
                        relu2(b * BSTEPS + s, (s - 1) % BSTEPS, None if first and s - 1 < R2 else b * (BSTEPS // 2) + ((s - 1) // 2 - 1))
                    if s % STEPS == 2 and not (first and h == 0):
                        copy_sim(b * HALVES + (h - 1), 1 - h, first)
                    if s % STEPS == 9 and not first:
                        exp_scores(b * HALVES + (h - 2))

            pair_batch(0, True)
            with act.Fori(1, NB) as b:
                pair_batch(b, False)
            relu2(NB * BSTEPS, BSTEPS - 1, NB * (BSTEPS // 2) - 2)
            copy_sim(NT - 1, 1, False)
            exp_scores(NT - 2)
            exp_scores(NT - 1)

            act.wait_ge(attn_step, AS * NT)
            act.wait_ge(l3_done, NT * GROUPS)

            def copy_xt(j, g):
                act.wait_ge(xt_done, j * GB + (g + 1))
                if g >= 2:
                    act.wait_ge(gu_done, j * GB + (g - 1))
                nc.scalar.activation(xTe[g % 2], ps_xt(g), ACT.Copy).then_inc(xt_copied, 1)

            with act.Fori(0, E // 2) as j:
                copy_xt(j, 0)
                for g in range(GB):
                    if g < GB - 1:
                        copy_xt(j, g + 1)
                    act.wait_ge(gu_done, j * GB + (g + 1))
                    if g >= 2:
                        act.wait_ge(mul_done, j * GB + (g - 1))
                    nc.scalar.activation(sge[g % 2][0:IM], ps_gate(g), ACT.Silu).then_inc(silu_done, 1)

            with act.Fori(0, NCH) as c:
                for m in range(JC):
                    w = min(P, J - m * P)
                    act.wait_ge(sgu_done, c * JC + (m + 1))
                    if m >= 2:
                        act.wait_ge(smul_done, c * JC + (m - 1))
                    nc.scalar.activation(sgs[m % 2][0:w], ps[0:w, 2 * (m % 2), :], ACT.Silu).then_inc(ssilu_done, 1)
                act.wait_ge(aoT_done, START + c + 1)
                act.wait_ge(sdown_done, START + c * CT)
                nc.scalar.activation(aoT[0:KD], ps[0:KD, 4, :], ACT.Copy).then_inc(aoT_copied, 1)

        @block.vector
        def _(dve):
            def layernorms(b, chunk):
                n = [0]

                def done(ins):
                    n[0] += 1
                    ins.then_inc(ln_step, 1)

                for r in range(2):
                    for h in range(HALVES):
                        dve.wait_ge(ln_step, START + b * LN + (n[0] if r == 0 else n[0] - 1))
                        src = xn1[:, ds(b * HALVES + h, 1), :] if r == 0 else xn1s[:, h:h + 1, :]
                        done(nc.vector.bn_stats(stats[:, r, h, :], src.rearrange("p o d -> p (o d)")))
                    for h in range(HALVES):
                        wait_alone(dve, "dve", ln_step, START + b * LN + (n[0] - 1))
                        done(nc.vector.bn_aggr(mv[:, r, h, :], stats[:, r, h, :]))
                    dve.wait_ge(ln_step, START + b * LN + n[0])
                    done(nc.vector.tensor_scalar(veps[:, r, :], mv[:, r, :, 1], EPS, None, ALU.add))
                    dve.wait_ge(rstd_ready, b * 2 + (r + 1))
                    if r == 0:
                        dve.wait_ge(t1_ready, START + b)
                        dve.wait_ge(xn1_kept, START + b)
                    else:
                        dve.wait_ge(t2_ready, START + b)
                    for h in range(HALVES):
                        src = xn1[:, ds(b * HALVES + h, 1), :] if r == 0 else xn1s[:, h:h + 1, :]
                        dst = (xn1s if r == 0 else xn2s)[:, h, :]
                        done(nc.vector.tensor_scalar(dst, src.rearrange("p o d -> p (o d)"), mv[:, r, h, 0:1],
                                                     rstd[:, r, h:h + 1], ALU.subtract, ALU.mult))

            def save_projections(b):
                dve.wait_ge(qkv_ready, START + b + 1)
                dve.wait_ge(kv_stored, START + b * 16)
                nc.vector.tensor_tensor(qao[:, ds(b * HALVES, HALVES), :], ps_qkv[:, :, 0:KD],
                                        bqkv[:, 0:KD].unsqueeze(1).to_broadcast([P, HALVES, KD]), ALU.add).then_inc(qkv_saved, 1)
                nc.vector.tensor_tensor(kvs, ps_qkv[:, :, KD:3 * KD],
                                        bqkv[:, KD:3 * KD].unsqueeze(1).to_broadcast([P, HALVES, 2 * KD]), ALU.add)\
                    .then_inc(qkv_saved, 1)
                nc.vector.tensor_copy(logits[:, ds(b * HALVES, HALVES), :], ps_logit).then_inc(qkv_saved, 1)

            dve.wait_ge(x_first_loaded, 16)
            layernorms(0, 0)
            dve.wait_ge(x_rest_loaded, 48)
            dve.wait_ge(consts_loaded, CONSTS)
            with dve.Fori(1, NB) as b:
                layernorms(b, 1)
                save_projections(b - 1)
            save_projections(NB - 1)

            steps = [0]

            def link(ins):
                steps[0] += 1
                ins.then_inc(route_step, 1)
                dve.wait_ge(route_step, steps[0])

            dve.wait_ge(made, 10)
            dve.wait_ge(qkv_saved, START + 3 * NB)
            for t in range(NT):
                nc.vector.max(best[:, t, :], logits[:, t, :]).then_inc(route_step, 1)
            steps[0] = NT
            dve.wait_ge(route_step, NT)
            link(nc.vector.tensor_tensor(dlog.rearrange("p (t o) -> p t o", o=1), best[:, :, 1:2], best[:, :, 0:1], ALU.subtract))
            dve.sem_inc(dlog_ready, 1)
            for t in range(NT):
                nc.vector.max_index(besti[:, t, :], best[:, t, :], logits[:, t, :]).then_inc(route_step, 1)
            steps[0] += NT
            dve.wait_ge(route_step, steps[0])
            link(nc.vector.tensor_copy(expert, besti[:, :, 0:2]))
            for k in range(2):
                link(nc.vector.tensor_tensor(hot[k], iota8[:, :].unsqueeze(1).to_broadcast([P, NT, E]),
                                             expert[:, :, k:k + 1].to_broadcast([P, NT, E]), ALU.is_equal))
            nc.vector.tensor_tensor(hots, hot[0], hot[1], ALU.add).then_inc(hot_ready, 1)
            dve.wait_ge(exp_routed, 1)
            link(nc.vector.tensor_scalar(eden, edlog, 1.0, None, ALU.add))
            w0 = route_w[:, :, 0:1].rearrange("p t o -> p (t o)")
            w1 = route_w[:, :, 1:2].rearrange("p t o -> p (t o)")
            link(nc.vector.reciprocal(w0, eden))
            link(nc.vector.tensor_tensor(w1, w0, edlog, ALU.mult))
            dve.wait_ge(counts_ready, 1)
            for e in range(E):
                link(nc.vector.tensor_tensor_scan(filled[:, :, e], ones[:, 0:NT], ps_count[:, :, e], 0.0, ALU.mult, ALU.add))
            link(nc.vector.tensor_tensor(base, filled, ps_count, ALU.subtract))
            link(nc.vector.tensor_tensor(base, base, ps_before, ALU.add))
            for k in range(2):
                link(nc.vector.tensor_tensor(hotpos[k], hot[k], base, ALU.mult))
                link(nc.vector.tensor_reduce(pos[:, :, k], hotpos[k], AX, ALU.add))
            link(nc.vector.tensor_scalar(posc, pos, float(CAP - 1), None, ALU.min))
            link(nc.vector.tensor_scalar(valid, pos, float(CAP), None, ALU.is_lt))
            link(nc.vector.tensor_scalar(over, pos, float(CAP), float(2 * SLOTS), ALU.is_ge, ALU.mult))
            link(nc.vector.scalar_tensor_tensor(slotf, expert, float(CAP), posc, ALU.mult, ALU.add))
            link(nc.vector.tensor_copy(slot_get[:, :, :], slotf))
            link(nc.vector.tensor_tensor(slot_put[:, :].rearrange("p (t k) -> p t k", k=2), slotf, over, ALU.add))
            link(nc.vector.tensor_tensor(route_w[:, :, :], route_w[:, :, :], valid, ALU.mult))
            dve.sem_inc(route_done, 1)

            dve.wait_ge(slots_zeroed, 16 * 5)
            dve.wait_ge(kv_stored, START + 16 * NB)
            dve.wait_ge(h_saved, START + 2 * NB)
            dve.wait_ge(xn1_kept, START + NB)
            dve.wait_ge(xT1_kept, START + NB)

            def relu1(b, s, first):
                if not (first and s < R1):
                    dve.wait_ge(l2_done, b * BSTEPS + (s - R1 + 1))
                rows = step_rows(s)
                for k in range(dve_rows(s)):
                    at = b * S + ((s // STEPS) * P + rows[k])
                    last = nc.vector.tensor_scalar(r1[:, s % R1, k, :], hneg[:, ds(b * S, S)], hb[:, ds(at, 1)], 0.0, ALU.add, ALU.max)
                last.then_inc(r1_dve, 1)

            zs = [z0, z1, z2, z1]

            def topk_round(t, h, b, r):
                n = t * TS + 4 * r
                if r == 0:
                    wait_alone(dve, "dve", diag_cleared, t + 1)
                else:
                    wait_alone(dve, "dve", topk_step, n)
                nc.vector.max(top8[:, r, :], zs[r]).then_inc(topk_step, 1)
                wait_alone(dve, "dve", topk_step, n + 1)
                nc.vector.max_index(idx8[:, r, :], top8[:, r, :], zs[r]).then_inc(topk_step, 1)
                if r < ROUNDS - 1:
                    nc.vector.match_replace(zs[r + 1], top8[:, r, :], zs[r], LOWEST).then_inc(topk_step, 1)
                dve.wait_ge(topk_step, n + 2)
                nc.vector.tensor_scalar(gidx[:, h, 8 * r:8 * r + 8], idx8[:, r, :], batch_row[:, ds(b, 1)], None, ALU.add)\
                    .then_inc(topk_step, 1)
                dve.wait_ge(topk_step, n + (4 if r < ROUNDS - 1 else 3))
                dve.sem_inc(idx_ready, 1)

            def attention(t, h, a):
                n = t * AS
                if a == 0:
                    dve.wait_ge(prod_ready, t + 1)
                    nc.vector.tensor_tensor(sc.rearrange("p r h -> p (r h)"),
                                            prod.rearrange("p r (h d) -> p (r h) d", d=2)[:, :, 0],
                                            prod.rearrange("p r (h d) -> p (r h) d", d=2)[:, :, 1], ALU.add).then_inc(attn_step, 1)
                elif a == 1:
                    dve.wait_ge(attn_step, n + 1)
                    nc.vector.tensor_reduce(smax[:, :], sc.rearrange("p r h -> p h r"), AX, ALU.max).then_inc(attn_step, 1)
                elif a == 2:
                    dve.wait_ge(attn_step, n + 2)
                    nc.vector.tensor_tensor(sc, sc, smax[:, :].unsqueeze(1).to_broadcast([P, TOPK, HEADS]), ALU.subtract)\
                        .then_inc(attn_step, 1)
                elif a == 3:
                    dve.wait_ge(exp_ready, t + 1)
                    nc.vector.tensor_reduce(sden[:, :], sc.rearrange("p r h -> p h r"), AX, ALU.add).then_inc(attn_step, 1)
                elif a == 4:
                    dve.wait_ge(attn_step, n + 4)
                    nc.vector.reciprocal(srec[:, :], sden[:, :]).then_inc(attn_step, 1)
                elif a == 5:
                    nc.vector.tensor_tensor(pv.rearrange("p r (h d) -> p r h d", d=2),
                                            kvg[:, h, :, KD:2 * KD].rearrange("p r (h d) -> p r h d", d=2),
                                            sc.unsqueeze(3).to_broadcast([P, TOPK, HEADS, 2]), ALU.mult).then_inc(attn_step, 1)
                elif a == 6:
                    dve.wait_ge(attn_step, n + 6)
                    nc.vector.tensor_reduce(aosum[:, :], pv.rearrange("p r k -> p k r"), AX, ALU.add).then_inc(attn_step, 1)
                elif a == 7:
                    dve.wait_ge(attn_step, n + 7)
                    nc.vector.tensor_tensor(qao[:, ds(t, 1), :].rearrange("p o (h d) -> p (o h) d", d=2),
                                            aosum[:, :].rearrange("p (h d) -> p h d", d=2),
                                            srec[:, :].unsqueeze(2).to_broadcast([P, HEADS, 2]), ALU.mult).then_inc(attn_step, 1)

            AT = {0: 0, 1: 1, 7: 2, 10: 3, 11: 4, 12: 5, 13: 6, 14: 7}
            TOP = {3: 0, 4: 1, 5: 2, 6: 3}

            def pair_batch(b, first):
                for s in range(BSTEPS):
                    h, s16 = s // STEPS, s % STEPS
                    relu1(b, s, first)
                    if s16 in AT and not first:
                        attention(b * HALVES + (h - 2), h, AT[s16])
                    if s16 in TOP and not (first and h == 0):
                        topk_round(b * HALVES + (h - 1), 1 - h, b if h else b - 1, TOP[s16])

            pair_batch(0, True)
            with dve.Fori(1, NB) as b:
                pair_batch(b, False)
            for r in range(ROUNDS):
                topk_round(NT - 1, 1, NB - 1, r)
            for t in (NT - 2, NT - 1):
                for a in range(AS):
                    attention(t, t % 2, a)

            dve.wait_ge(l3_done, NT * GROUPS)

            def gate_times_up(j, g):
                dve.wait_ge(silu_done, j * GB + (g + 1))
                if g >= 2:
                    dve.wait_ge(down_done, j * GB + (g - 1))
                nc.vector.tensor_tensor(hTe[g % 2][0:IM], sge[g % 2][0:IM], ps_up(g), ALU.mult).then_inc(mul_done, 1)

            def copy_down(j, g):
                i = g // GPE
                dve.wait_ge(down_done, j * GB + (g + 1))
                if g % GPE == 0:
                    dve.wait_ge(y_stored[i], START + j * 16)
                n0 = 2 * (g % GPE)
                nc.vector.tensor_copy(oute[i][:, n0:n0 + 2, :], ps_down(g)).then_inc(down_copied, 1)

            with dve.Fori(0, E // 2) as j:
                for g in range(GB):
                    gate_times_up(j, g)
                    if g:
                        copy_down(j, g - 1)
                copy_down(j, GB - 1)

            with dve.Fori(0, NCH) as c:
                dve.wait_ge(sdown_done, START + c * CT)
                for m in range(JC):
                    w = min(P, J - m * P)
                    dve.wait_ge(ssilu_done, c * JC + (m + 1))
                    nc.vector.tensor_tensor(hTs[0:w, m, :], sgs[m % 2][0:w], ps[0:w, 2 * (m % 2) + 1, :], ALU.mult)\
                        .then_inc(smul_done, 1)
                dve.wait_ge(ys_gathered, c * (16 * 2 * CT) + 16 * 2 * CT)
                dve.wait_ge(out_stored, START + c * 16)
                for n in range(CT):
                    dve.wait_ge(sdown_done, START + c * CT + (n // 2 * 2 + 2))
                    nc.vector.scalar_tensor_tensor(fin[:, n, :], ys[:, n, 0, :], route_w[:, ds(c * CT + n, 1), 0:1].rearrange("p a b -> p (a b)"),
                                                   ps[:, 6 + n // 2, (n % 2) * D:(n % 2 + 1) * D], ALU.mult, ALU.add)\
                        .then_inc(comb_step, 1)
                for n in range(CT):
                    dve.wait_ge(comb_step, START + c * CS + (n + 1))
                    nc.vector.scalar_tensor_tensor(fin[:, n, :], ys[:, n, 1, :], route_w[:, ds(c * CT + n, 1), 1:2].rearrange("p a b -> p (a b)"),
                                                   fin[:, n, :], ALU.mult, ALU.add).then_inc(comb_step, 1)
                dve.wait_ge(resid_ready, c * 2 + 2)
                for n in range(CT):
                    dve.wait_ge(comb_step, START + c * CS + (CT + n + 1))
                    nc.vector.tensor_tensor(fin[:, n, :], fin[:, n, :], resid[:, n, :], ALU.add).then_inc(comb_step, 1)


_PRE = "L0_attn_"
_INS = [("L0_attn_x", False), ("L0_attn_gamma", False), ("L0_attn_beta", False), ("L0_attn_W1", True), ("L0_attn_b1", False),
        ("L0_attn_W2", True), ("L0_attn_b2", False), ("L0_attn_W3", False), ("L0_attn_b3", False), ("L0_attn_Wqkv", True),
        ("L0_attn_bqkv", False), ("L0_attn_Wout", True), ("L0_attn_bout", False), ("L0_ffn_router", False),
        ("L0_ffn_w_up_gate", False), ("L0_ffn_w_down", False), ("L0_ffn_shared_w_up_gate", False),
        ("L0_ffn_shared_w_down", False)]
_OUTS = [((16, 256, 256), "float32")]


def kernel(**inputs):
    import numpy as _np
    import concourse.bacc as _bacc
    from concourse import mybir as _mybir
    from concourse.bass_utils import run_bass_kernel_spmd as _run

    nc = _bacc.Bacc("TRN2", target_bir_lowering=False, num_devices=1)
    arrays, args = {}, []
    for name, transposed in _INS:
        a = _np.asarray(inputs[name])
        a = _np.ascontiguousarray(a.T if transposed else a)
        arrays[f"in_{name}_dram"] = a
        args.append(nc.dram_tensor(f"in_{name}_dram", a.shape, _mybir.dt.from_np(a.dtype), kind="ExternalInput").ap())
    for i, (shape, dtype) in enumerate(_OUTS):
        dt = _mybir.dt.from_np(_np.dtype(dtype))
        args.append(nc.dram_tensor(f"out_{i}_dram", shape, dt, kind="ExternalOutput").ap())
    lsn_attention_moe_block(nc, *args)
    r = _run(nc, [arrays], core_ids=[0])
    got = tuple(r.results[0][f"out_{i}_dram"] for i in range(len(_OUTS)))
    return got[0]
```

```python
import concourse.bass as bass
from concourse import mybir
from contextlib import ExitStack


def lsn_attention_moe_block(
    nc: bass.Bass,
    x_d: bass.AP,
    gamma_d: bass.AP,
    beta_d: bass.AP,
    w1t_d: bass.AP,
    b1_d: bass.AP,
    w2t_d: bass.AP,
    b2_d: bass.AP,
    w3_d: bass.AP,
    b3_d: bass.AP,
    wqkvt_d: bass.AP,
    bqkv_d: bass.AP,
    woutt_d: bass.AP,
    bout_d: bass.AP,
    router_d: bass.AP,
    wug_d: bass.AP,
    wdn_d: bass.AP,
    swug_d: bass.AP,
    swdn_d: bass.AP,
    out_d: bass.AP,
):
    f32 = mybir.dt.float32
    u32 = mybir.dt.uint32
    ALU = mybir.AluOpType
    ACT = mybir.ActivationFunctionType
    AX = mybir.AxisListType.X
    ds = bass.ds

    P = 128
    NB, S, D = x_d.shape
    DC = D // P
    NT = NB * S // P
    HALVES = S // P
    F1, G2 = w2t_d.shape
    KD = woutt_d.shape[0]
    HEADS, HD = 32, KD // 32
    TOPK = max(1, int(S * 0.1))
    ROUNDS = (TOPK + 7) // 8
    EPS = 1e-5
    SCALE = float(HD) ** -0.5
    E = router_d.shape[1]
    TOKENS = NB * S
    CAP = -(-TOKENS * 2 * 5 // (E * 4))
    SLOTS = E * CAP
    I = wdn_d.shape[1]
    TAIL = 64
    IM = I - TAIL
    J = swdn_d.shape[0]
    JC = (J - TAIL) // P
    LOWEST = -3.0e38

    UNIT = 4
    STEP_ROWS = 2 * UNIT
    STEPS = P // STEP_ROWS
    BSTEPS = HALVES * STEPS
    R1 = 4
    R2 = 4

    NPE = CAP // P
    GPE = NPE // 2
    GB = 2 * GPE
    CT = 4
    NCH = NT // CT

    x_t = x_d.rearrange("b (h p) d -> p (b h) d", p=P)
    out_t = out_d.rearrange("b (h p) d -> p (b h) d", p=P)
    kv_dram = nc.dram_tensor("kv_rows", (TOKENS, 2 * KD), f32, kind="Internal").ap()
    slot_dram = nc.dram_tensor("slot_inputs", (SLOTS, D), f32, kind="Internal").ap()
    yslot_dram = nc.dram_tensor("slot_outputs", (SLOTS, D), f32, kind="Internal").ap()

    ctx = ExitStack()
    with ctx:
        def sb(name, shape, dt=f32):
            return ctx.enter_context(nc.sbuf_tensor(name, shape, dt))

        def sem(name):
            return ctx.enter_context(nc.semaphore(name))

        xn1 = sb("xn1", [P, NT, D])
        xT1 = sb("xT1", [P, DC, TOKENS])
        qao = sb("qao", [P, NT, KD])
        w1t = sb("w1t", [P, DC, F1])
        wqkvt = sb("wqkvt", [P, DC, 3 * KD])
        router = sb("router", [P, DC, E])
        w2t = sb("w2t", [F1, G2])
        w3win = sb("w3win", [2 * G2, 64])
        gamma = sb("gamma", [P, DC])
        beta = sb("beta", [P, DC])
        b1 = sb("b1", [F1, 1])
        b2 = sb("b2", [2 * G2, 1])
        b3 = sb("b3", [P, 1])
        bqkv = sb("bqkv", [P, 3 * KD])
        bout = sb("bout", [P, D])
        ident = sb("ident", [P, P])
        earlier = sb("earlier", [P, P])
        ones = sb("ones", [P, P])
        iota8 = sb("iota8", [P, E])
        batch_row = sb("batch_row", [P, NB])
        route_w = sb("route_w", [P, NT, 2])
        slot_get = sb("slot_get", [P, NT, 2], u32)
        slot_put = sb("slot_put", [P, NT * 2], u32)

        ARENA = 31392
        arena = sb("arena", [P, ARENA])
        taken = [0]

        def part(n, *dims):
            at = taken[0]
            taken[0] = at + n
            assert taken[0] <= ARENA
            view = arena[:, at:at + n]
            if len(dims) == 1:
                return view.rearrange("p (a b) -> p a b", a=dims[0])
            if len(dims) == 2:
                return view.rearrange("p (a b c) -> p a b c", a=dims[0], b=dims[1])
            return view

        hneg = part(TOKENS)
        hb = part(TOKENS)
        rows_base = taken[0]
        r1 = part(R1 * STEP_ROWS * S, R1, STEP_ROWS)
        r2 = part(R2 * 2 * 512, R2)
        attn_base = taken[0]
        kvg = part(2 * TOPK * 2 * KD, 2, TOPK)
        prod = part(TOPK * KD, TOPK)
        sc = part(TOPK * HEADS, TOPK)
        pv = part(TOPK * KD, TOPK)
        z0 = part(S)
        z1 = part(S)
        pair_end = taken[0]
        top8 = sb("top8", [P, ROUNDS, 8])
        idx8 = sb("idx8", [P, ROUNDS, 8], u32)
        gidx = sb("gidx", [P, 2, ROUNDS * 8], u32)
        smax = sb("smax", [P, HEADS])
        sden = sb("sden", [P, HEADS])
        srec = sb("srec", [P, HEADS])
        aosum = sb("aosum", [P, KD])

        taken[0] = rows_base
        xn1s = part(HALVES * D, HALVES)
        xn2s = part(HALVES * D, HALVES)
        xT1s = part(DC * S, DC)
        xn2T = part(DC * S, DC)
        kvs = part(HALVES * 2 * KD, HALVES)
        stats = part(2 * HALVES * 6, 2, HALVES)
        mv = part(2 * HALVES * 2, 2, HALVES)
        veps = part(2 * HALVES, 2)
        rstd = part(2 * HALVES, 2)
        neg_half = part(HALVES)
        zeros = part(SLOTS // P * D // 5)
        assert taken[0] <= attn_base
        taken[0] = attn_base + TOPK * 2 * KD
        logits = part(NT * E, NT)
        best = part(NT * E, NT)
        besti = part(NT * E, NT).bitcast(u32)
        expert = part(NT * 2, NT)
        dlog = part(NT)
        edlog = part(NT)
        eden = part(NT)
        hot = [part(NT * E, NT) for _ in range(2)]
        hots = part(NT * E, NT)
        filled = part(NT * E, NT)
        base = part(NT * E, NT)
        hotpos = [part(NT * E, NT) for _ in range(2)]
        pos = part(NT * 2, NT)
        posc = part(NT * 2, NT)
        slotf = part(NT * 2, NT)
        over = part(NT * 2, NT)
        valid = part(NT * 2, NT)
        assert taken[0] <= attn_base + 2 * TOPK * 2 * KD

        taken[0] = 0
        xe = [part(NPE * D, NPE) for _ in range(2)]
        wug = [part(DC * 2 * I, DC) for _ in range(2)]
        wdn = [part(2 * D, 2) for _ in range(2)]
        xTe = [part(DC * 256, DC) for _ in range(2)]
        sge = [part(2 * 256, 2) for _ in range(2)]
        hTe = [part(2 * 256, 2) for _ in range(2)]
        oute = [part(NPE * D, NPE) for _ in range(2)]
        swug = part(DC * 2 * J, DC)
        swdn = part((JC + 1) * D, JC + 1)
        assert taken[0] <= attn_base
        taken[0] = attn_base
        sgs = [part(512) for _ in range(2)]
        hTs = part((JC + 1) * 512, JC + 1)
        aos = part(CT * KD, CT)
        ys = part(CT * 2 * D, CT, 2)
        resid = part(CT * D, CT)
        fin = part(CT * D, CT)
        ysidx = sb("ysidx", [P, CT, 2], u32)
        xstage = sb("xstage", [P, HALVES, D])
        istage = sb("istage", [P, HALVES * 2], u32)

        ps = ctx.enter_context(nc.psum_tensor("ps", [P, 8, 512], f32))

        ps_t1 = ps[:, 0, :].rearrange("p (c s) -> p c s", c=DC)
        ps_t2 = ps[:, 1, :].rearrange("p (c s) -> p c s", c=DC)
        ps_h = ps[:, 2, 0:S]
        ps_qkv = ps[:, 3, :].rearrange("p (h n) -> p h n", h=HALVES)
        ps_logit = ps[:, 4, 0:HALVES * E].rearrange("p (h n) -> p h n", h=HALVES)
        ps_before = ps[:, 7, 0:NT * E].rearrange("p (t e) -> p t e", e=E)
        ps_count = ps[:, 7, NT * E:2 * NT * E].rearrange("p (t e) -> p t e", e=E)

        PS2 = 3

        def ps_l2(s):
            return ps[:, 2 * (s % PS2):2 * (s % PS2) + 2, :]

        def ps2_before(s):
            if s >= PS2:
                return s - PS2
            return max(x for x in range(BSTEPS) if x % PS2 == s) - BSTEPS

        def ps_sim(h):
            return ps[:, 6 + h, 0:S]

        def ps_xt(g):
            return ps[:, 6 + g % 2, :].rearrange("p (c n) -> p c n", c=DC)

        def ps_gate(g):
            return ps[0:IM, 2 * (g % 2), 0:256]

        def ps_up(g):
            return ps[0:IM, 2 * (g % 2) + 1, 0:256]

        def ps_tail(g):
            return ps[:, 2 * (g % 2), 256:512]

        def ps_down(g):
            return ps[:, 4 + g % 2, :].rearrange("p (n d) -> p n d", n=2)

        consts_loaded = sem("consts_loaded")
        x_first_loaded = sem("x_first_loaded")
        x_rest_loaded = sem("x_rest_loaded")
        made = sem("made")
        ln_step = sem("ln_step")
        rstd_ready = sem("rstd_ready")
        t1_ready = sem("t1_ready")
        t2_ready = sem("t2_ready")
        xT1s_ready = sem("xT1s_ready")
        xn2T_ready = sem("xn2T_ready")
        h_ready = sem("h_ready")
        h_saved = sem("h_saved")
        qkv_ready = sem("qkv_ready")
        qkv_saved = sem("qkv_saved")
        kv_stored = sem("kv_stored")
        staged = sem("staged")
        xT1_kept = sem("xT1_kept")
        slots_zeroed = sem("slots_zeroed")
        route_step = sem("route_step")
        hot_ready = sem("hot_ready")
        dlog_ready = sem("dlog_ready")
        exp_routed = sem("exp_routed")
        counts_ready = sem("counts_ready")
        route_done = sem("route_done")
        scattered = sem("scattered")

        r1_dve = sem("r1_dve")
        r1_act = sem("r1_act")
        l2_done = sem("l2_done")
        r2_done = sem("r2_done")
        l3_done = sem("l3_done")
        sim_copied = sem("sim_copied")
        diag_cleared = sem("diag_cleared")
        topk_step = sem("topk_step")
        idx_ready = sem("idx_ready")
        gathered = sem("gathered")
        prod_ready = sem("prod_ready")
        attn_step = sem("attn_step")
        exp_ready = sem("exp_ready")

        xe_loaded = [sem(f"xe_loaded{i}") for i in range(2)]
        we_loaded = [sem(f"we_loaded{i}") for i in range(2)]
        xt_done = sem("xt_done")
        xt_copied = sem("xt_copied")
        gu_done = sem("gu_done")
        silu_done = sem("silu_done")
        mul_done = sem("mul_done")
        down_done = sem("down_done")
        down_copied = sem("down_copied")
        y_stored = [sem(f"y_stored{i}") for i in range(2)]

        shared_loaded = sem("shared_loaded")
        sgu_done = sem("sgu_done")
        ssilu_done = sem("ssilu_done")
        smul_done = sem("smul_done")
        ao_fetched = sem("ao_fetched")
        aoT_done = sem("aoT_done")
        aoT_copied = sem("aoT_copied")
        sdown_done = sem("sdown_done")
        ysidx_ready = sem("ysidx_ready")
        ys_gathered = sem("ys_gathered")
        resid_loaded = sem("resid_loaded")
        resid_ready = sem("resid_ready")
        comb_step = sem("comb_step")
        out_stored = sem("out_stored")

        START = 1
        started = [ln_step, t1_ready, t2_ready, xT1s_ready, xn2T_ready, h_saved, qkv_ready, qkv_saved, kv_stored, 
                   xT1_kept, down_copied, y_stored[0], y_stored[1], comb_step, aoT_done, aoT_copied, sdown_done, out_stored]

        N_CONST = 12 + 2 * DC
        CONSTS = 16 * N_CONST
        LN1 = 4 * HALVES + 1
        LN = LN1 + 3 * HALVES + 1
        TS = 3 * ROUNDS - 1
        AS = 8
        CS = 3 * CT

        GROUPS = STEPS // 2

        def dve_rows(s):
            return 6 if s % STEPS < 4 else 5

        passed = {name: sem(f"{name}_passed") for name in ("dve", "pe", "pool")}

        def wait_alone(eng, name, what, value):
            eng.wait_ge(what, value)
            eng.sem_inc(passed[name], 1)

        block = ctx.enter_context(nc.Block())

        @block.sync
        def _(sp):
            sp.dma_start(xn1[:, 0:HALVES, :], x_t[:, 0:HALVES, :]).then_inc(x_first_loaded, 16)
            for s in started:
                sp.sem_inc(s, START)
            for dst, src in (
                (w1t[:, :, :], w1t_d.rearrange("(c p) f -> p c f", p=P)),
                (wqkvt[:, :, :], wqkvt_d.rearrange("(c p) f -> p c f", p=P)),
                (router[:, :, :], router_d.rearrange("(c p) f -> p c f", p=P)),
                *((to[:, c:c + 1], src[c * P:(c + 1) * P].rearrange("(p o) -> p o", o=1))
                  for to, src in ((gamma, gamma_d), (beta, beta_d)) for c in range(DC)),
                (b1[:, :], b1_d.rearrange("(p o) -> p o", o=1)),
                (bqkv[:, :], bqkv_d.partition_broadcast(P)),
                (w2t[:, :], w2t_d),
                (b2[0:G2, :], b2_d.rearrange("(p o) -> p o", o=1)),
                (b2[G2:2 * G2, :], b2_d.rearrange("(p o) -> p o", o=1)),
                (b3[:, :], b3_d.partition_broadcast(P)),
                (bout[:, :], bout_d.partition_broadcast(P)),
            ):
                sp.dma_start(dst, src).then_inc(consts_loaded, 16)
            sp.wait_ge(made, 1)
            sp.dma_start(w3win[0:G2, 32:33], w3_d.rearrange("o g -> g o")).then_inc(consts_loaded, 16)
            sp.dma_start(w3win[G2:2 * G2, 34:35], w3_d.rearrange("o g -> g o")).then_inc(consts_loaded, 16)
            rest = NT - HALVES
            for i in range(3):
                a, b = HALVES + rest * i // 3, HALVES + rest * (i + 1) // 3
                sp.dma_start(xn1[:, a:b, :], x_t[:, a:b, :]).then_inc(x_rest_loaded, 16)
            sp.wait_ge(made, 2)
            zv = slot_dram.rearrange("(k p n) d -> k p (n d)", k=5, p=P)
            for k in range(5):
                sp.dma_start(zv[k], zeros).then_inc(slots_zeroed, 16)
            with sp.Fori(0, NB) as b:
                sp.wait_ge(qkv_saved, START + b * 3 + 3)
                sp.dma_start(kv_dram[ds(b * S, S), :].rearrange("(h p) n -> p h n", p=P), kvs)\
                  .then_inc(kv_stored, 16)

            sp.wait_ge(route_done, 1)
            sp.wait_ge(ln_step, START + NB * LN)

            def stage(b):
                sp.dma_start(xstage[:, :, :], xn1[:, ds(b * HALVES, HALVES), :]).then_inc(staged, 16)
                sp.dma_start(istage[:, :], slot_put[:, ds(b * (HALVES * 2), HALVES * 2)]).then_inc(staged, 16)

            stage(0)
            with sp.Fori(1, NB) as b:
                sp.wait_ge(scattered, b * (16 * 2 * HALVES))
                stage(b)

            sp.wait_ge(l3_done, NT * GROUPS)
            sp.wait_ge(scattered, 16 * 2 * NT)

            def load_expert(e, i):
                sp.dma_start(xe[i], slot_dram[ds(e * CAP, CAP), :].rearrange("(p n) d -> p n d", p=P))\
                  .then_inc(xe_loaded[i], 16)
                sp.dma_start(wug[i], wug_d[ds(e, 1), :, :].rearrange("o (c p) m -> p (o c) m", p=P))\
                  .then_inc(we_loaded[i], 16)
                sp.dma_start(wdn[i][0:IM, 0, :], wdn_d[ds(e, 1), 0:IM, :].rearrange("o p d -> p (o d)"))\
                  .then_inc(we_loaded[i], 16)
                sp.dma_start(wdn[i][TAIL:2 * TAIL, 1, :], wdn_d[ds(e, 1), IM:I, :].rearrange("o p d -> p (o d)"))\
                  .then_inc(we_loaded[i], 16)

            def store_expert(e, i, last_group):
                sp.wait_ge(down_copied, START + last_group)
                sp.dma_start(yslot_dram[ds(e * CAP, CAP), :].rearrange("(p n) d -> p n d", p=P), oute[i])\
                  .then_inc(y_stored[i], 16)

            for i in range(2):
                load_expert(i, i)
            sp.dma_start(swug, swug_d.rearrange("(c p) m -> p c m", p=P)).then_inc(shared_loaded, 16)
            sp.dma_start(swdn[:, 0:JC, :], swdn_d[0:JC * P, :].rearrange("(c p) d -> p c d", p=P))\
              .then_inc(shared_loaded, 16)
            sp.dma_start(swdn[0:KD, JC, :], woutt_d).then_inc(shared_loaded, 16)
            sp.dma_start(swdn[KD:KD + TAIL, JC, :], swdn_d[JC * P:J, :]).then_inc(shared_loaded, 16)
            with sp.Fori(0, E // 2 - 1) as j:
                for i in range(2):
                    sp.wait_ge(down_done, j * GB + GPE * (i + 1))
                    load_expert(j * 2 + (2 + i), i)
                    store_expert(j * 2 + i, i, j * GB + GPE * (i + 1))
            for i in range(2):
                store_expert(E - 2 + i, i, GB * (E // 2 - 1) + GPE * (i + 1))

            sp.wait_ge(attn_step, AS * NT)

            def load_resid(c):
                sp.wait_ge(comb_step, START + c * CS)
                sp.dma_start(resid, x_t[:, ds(c * CT, CT), :]).then_inc(resid_loaded, 16)

            load_resid(0)
            with sp.Fori(0, NCH - 1) as c:
                load_resid(c + 1)
                sp.dma_start(out_t[:, ds(c * CT, CT), :], fin).then_inc(out_stored, 16)
            sp.wait_ge(comb_step, START + NCH * CS)
            sp.dma_start(out_t[:, (NCH - 1) * CT:NCH * CT, :], fin).then_inc(out_stored, 16)
            sp.wait_ge(out_stored, START + 16 * NCH)

        @block.gpsimd
        def _(pool):
            nc.gpsimd.memset(w3win[:, :], 0.0).then_inc(made, 1)
            nc.gpsimd.memset(zeros, 0.0).then_inc(made, 1)
            nc.gpsimd.memset(ident[:, :], 0.0).then_inc(made, 1)
            nc.gpsimd.memset(earlier[:, :], 1.0).then_inc(made, 1)
            nc.gpsimd.memset(ones[:, :], 1.0).then_inc(made, 1)
            nc.gpsimd.memset(neg_half, -0.5).then_inc(made, 1)
            pool.wait_ge(made, 6)
            nc.gpsimd.affine_select(out=ident[:, :], in_=ident[:, :], compare_op=ALU.not_equal, fill=1.0, base=0,
                                    pattern=[[-1, P]], channel_multiplier=1).then_inc(made, 1)
            nc.gpsimd.affine_select(out=earlier[:, :], in_=earlier[:, :], compare_op=ALU.is_gt, fill=0.0, base=0,
                                    pattern=[[1, P]], channel_multiplier=-1).then_inc(made, 1)
            nc.gpsimd.iota(iota8[:, :], pattern=[[1, E]], base=0, channel_multiplier=0,
                           allow_small_or_imprecise_dtypes=True).then_inc(made, 1)
            nc.gpsimd.iota(batch_row[:, :], pattern=[[S, NB]], base=0, channel_multiplier=0,
                           allow_small_or_imprecise_dtypes=True).then_inc(made, 1)

            with pool.Fori(0, NB) as b:
                for r in range(2):
                    pool.wait_ge(ln_step, START + b * LN + (r * LN1 + 2 * HALVES + 1))
                    nc.gpsimd.tensor_tensor(rstd[:, r, :], veps[:, r, :], neg_half, ALU.pow).then_inc(rstd_ready, 1)

            pool.wait_ge(kv_stored, START + 16 * NB)
            pool.wait_ge(slots_zeroed, 16 * 5)

            def scatter_tile(b, h):
                if h == 0:
                    wait_alone(pool, "pool", staged, b * 32 + 32)
                for k in range(2):
                    pool.indirect_dma_start(
                        out=slot_dram, out_offset=bass.IndirectOffsetOnAxis(ap=istage[:, 2 * h + k:2 * h + k + 1], axis=0),
                        in_=xstage[:, h, :], in_offset=None, bounds_check=SLOTS - 1, oob_is_err=False).then_inc(scattered, 16)

            def gather_tile(t, h, first):
                wait_alone(pool, "pool", sim_copied, t + 1)
                nc.gpsimd.affine_select(out=z0, in_=z0, compare_op=ALU.not_equal, fill=0.0, base=P * h,
                                        pattern=[[-1, S]], channel_multiplier=1).then_inc(diag_cleared, 1)
                if not first:
                    wait_alone(pool, "pool", attn_step, (t - 1) * AS)
                for r in range(TOPK):
                    if r % 8 == 0:
                        wait_alone(pool, "pool", idx_ready, t * ROUNDS + (r // 8 + 1))
                    pool.indirect_dma_start(
                        out=kvg[:, h, r, :], out_offset=None, in_=kv_dram,
                        in_offset=bass.IndirectOffsetOnAxis(ap=gidx[:, h, r:r + 1], axis=0)).then_inc(gathered, 16)
                pool.wait_ge(gathered, (t + 1) * (16 * TOPK))
                if not (first and h == 0):
                    pool.wait_ge(attn_step, (t - 1) * AS + 1)
                nc.gpsimd.tensor_tensor(prod, kvg[:, h, :, 0:KD],
                                        qao[:, ds(t, 1), :].to_broadcast([P, TOPK, KD]), ALU.mult)\
                    .then_inc(prod_ready, 1)

            for h in range(HALVES):
                scatter_tile(0, h)
                gather_tile(h, h, True)
            with pool.Fori(1, NB) as b:
                for h in range(HALVES):
                    scatter_tile(b, h)
                    gather_tile(b * HALVES + h, h, False)

            pool.wait_ge(attn_step, AS * NT)
            pool.wait_ge(y_stored[0], START + 16 * (E // 2))
            pool.wait_ge(y_stored[1], START + 16 * (E // 2))
            with pool.Fori(0, NCH) as c:
                pool.wait_ge(comb_step, START + c * CS)
                pool.wait_ge(aoT_done, START + c)
                nc.gpsimd.tensor_copy(aos, qao[:, ds(c * CT, CT), :]).then_inc(ao_fetched, 1)
                nc.gpsimd.tensor_copy(ysidx[:, :, :], slot_get[:, ds(c * CT, CT), :]).then_inc(ysidx_ready, 1)
                wait_alone(pool, "pool", ysidx_ready, c + 1)
                for n in range(CT):
                    for k in range(2):
                        pool.indirect_dma_start(
                            out=ys[:, n, k, :], out_offset=None, in_=yslot_dram,
                            in_offset=bass.IndirectOffsetOnAxis(ap=ysidx[:, n, k:k + 1], axis=0)).then_inc(ys_gathered, 16)
                pool.wait_ge(resid_loaded, c * 16 + 16)
                nc.gpsimd.tensor_tensor(resid, resid, xn1[:, ds(c * CT, CT), :], ALU.add).then_inc(resid_ready, 1)
                pool.wait_ge(resid_ready, c * 2 + 1)
                nc.gpsimd.tensor_tensor(resid, resid, bout[:, :].unsqueeze(1).to_broadcast([P, CT, D]), ALU.add)\
                    .then_inc(resid_ready, 1)

        @block.tensor
        def _(pe):
            pe.wait_ge(consts_loaded, CONSTS)
            pe.wait_ge(made, 10)
            with pe.Fori(0, NB) as b:
                pe.wait_ge(ln_step, START + b * LN + (LN1 - HALVES))
                pe.wait_ge(xT1_kept, START + b)
                for h in range(HALVES):
                    for c in range(DC):
                        last = nc.tensor.transpose(ps_t1[:, c, h * P:(h + 1) * P], xn1s[:, h, c * P:(c + 1) * P], ident[:, :])
                last.then_inc(t1_ready, 1)
                pe.wait_ge(ln_step, START + b * LN + LN)
                pe.wait_ge(xn2T_ready, START + b * DC)
                for h in range(HALVES):
                    for c in range(DC):
                        last = nc.tensor.transpose(ps_t2[:, c, h * P:(h + 1) * P], xn2s[:, h, c * P:(c + 1) * P], ident[:, :])
                last.then_inc(t2_ready, 1)
                pe.wait_ge(xT1s_ready, START + b + 1)
                pe.wait_ge(qkv_saved, START + b * 3)
                for h in range(HALVES):
                    for c in range(DC):
                        nc.tensor.matmul(ps_logit[:, h, :], xT1s[:, c, h * P:(h + 1) * P], router[:, c, :],
                                         start=(c == 0), stop=(c == DC - 1))
                pe.wait_ge(xn2T_ready, START + b * DC + DC)
                pe.wait_ge(h_saved, START + b * 2)
                for c in range(DC):
                    last = nc.tensor.matmul(ps_h, w1t[:, c, :], xn2T[:, c, :], start=(c == 0), stop=(c == DC - 1))
                last.then_inc(h_ready, 1)
                for h in range(HALVES):
                    for c in range(DC):
                        last = nc.tensor.matmul(ps_qkv[:, h, 0:3 * KD], xn2T[:, c, h * P:(h + 1) * P], wqkvt[:, c, :],
                                                start=(c == 0), stop=(c == DC - 1))
                last.then_inc(qkv_ready, 1)

            pe.wait_ge(h_saved, START + 2 * NB)
            pe.wait_ge(qkv_saved, START + 3 * NB)

            def count_choices():
                pe.wait_ge(hot_ready, 1)
                hv = hots.rearrange("p t e -> p (t e)")
                nc.tensor.matmul(ps[:, 7, 0:NT * E], earlier[:, :], hv, start=True, stop=True)
                nc.tensor.matmul(ps[:, 7, NT * E:2 * NT * E], ones[:, :], hv, start=True, stop=True).then_inc(counts_ready, 1)

            def layer2(b, s, first):
                pe.wait_ge(r1_dve, b * BSTEPS + (s + 1))
                pe.wait_ge(r1_act, b * BSTEPS + (s + 1))
                if not (first and s < PS2):
                    pe.wait_ge(r2_done, b * BSTEPS + (ps2_before(s) + 1))
                for u in range(2):
                    for v in range(2):
                        last = nc.tensor.matmul(ps_l2(s)[v * G2:(v + 1) * G2, u, :], w2t[:, :],
                                                r1[:, s % R1, 4 * u + 2 * v:4 * u + 2 * v + 2, :], start=True, stop=True)
                last.then_inc(l2_done, 1)

            def layer3(steps, s):
                pe.wait_ge(r2_done, steps)
                q, h = s % STEPS // 2, s // STEPS
                for a in range(2):
                    for c in range(4):
                        at = 32 - (UNIT * q + a)
                        last = nc.tensor.matmul(ps_sim(h)[32 * c:32 * c + 32, :], w3win[:, at:at + 32],
                                                r2[:, (s - 1 + c // 2) % R2, 512 * (c % 2) + a * S:512 * (c % 2) + (a + 1) * S],
                                                start=(q == 0 and a == 0), stop=(q == GROUPS - 1 and a == 1))
                last.then_inc(l3_done, 1)

            def pair_batch(b, first):
                for s in range(BSTEPS):
                    layer2(b, s, first)
                    if first and s == 8:
                        count_choices()
                    if first and s == STEPS:
                        pe.wait_ge(route_done, 1)
                    if s == 1 and not first:
                        layer3(b * BSTEPS, BSTEPS - 1)
                    elif s % 2 == 1 and s > 1:
                        if s % STEPS == 3 and not first:
                            pe.wait_ge(sim_copied, b * HALVES + (s // STEPS - 1))
                        layer3(b * BSTEPS + (s - 1), s - 2)

            pair_batch(0, True)
            with pe.Fori(1, NB) as b:
                pair_batch(b, False)
            layer3(NB * BSTEPS, BSTEPS - 1)

            pe.wait_ge(sim_copied, NT)

            def transpose_slots(j, g):
                if g >= 2:
                    pe.wait_ge(xt_copied, j * GB + (g - 1))
                i, n0 = g // GPE, 2 * (g % GPE)
                if g % GPE == 0:
                    pe.wait_ge(xe_loaded[i], j * 16 + 16)
                for n in range(2):
                    for c in range(DC):
                        last = nc.tensor.transpose(ps_xt(g)[:, c, n * P:(n + 1) * P],
                                                   xe[i][:, n0 + n, c * P:(c + 1) * P], ident[:, :])
                last.then_inc(xt_done, 1)

            def gate_up(j, g):
                i = g // GPE
                if g % GPE == 0:
                    pe.wait_ge(we_loaded[i], j * 48 + 48)
                pe.wait_ge(xt_copied, j * GB + (g + 1))
                if g >= 2:
                    pe.wait_ge(mul_done, j * GB + (g - 1))
                for to, col, w in ((ps_gate(g), 0, IM), (ps_up(g), IM, IM), (ps_tail(g), 2 * IM, 2 * TAIL)):
                    for c in range(DC):
                        last = nc.tensor.matmul(to, wug[i][:, c, col:col + w], xTe[g % 2][:, c, :],
                                                start=(c == 0), stop=(c == DC - 1))
                last.then_inc(gu_done, 1)

            def down(j, g):
                pe.wait_ge(mul_done, j * GB + (g + 1))
                if g >= 2:
                    pe.wait_ge(down_copied, START + j * GB + (g - 1))
                for n in range(2):
                    for m, rows in enumerate((slice(0, IM), slice(TAIL, 2 * TAIL))):
                        last = nc.tensor.matmul(ps_down(g)[:, n, :], hTe[g % 2][rows, m, n * P:(n + 1) * P],
                                                wdn[g // GPE][rows, m, :], start=(m == 0), stop=(m == 1))
                last.then_inc(down_done, 1)

            with pe.Fori(0, E // 2) as j:
                pe.wait_ge(down_copied, START + j * GB)
                transpose_slots(j, 0)
                for g in range(GB):
                    if g < GB - 1:
                        transpose_slots(j, g + 1)
                    gate_up(j, g)
                    if g:
                        down(j, g - 1)
                down(j, GB - 1)

            pe.wait_ge(shared_loaded, 16 * 4)
            pe.wait_ge(down_copied, START + GB * (E // 2))
            with pe.Fori(0, NCH) as c:
                for m in range(JC):
                    if m >= 2:
                        wait_alone(pe, "pe", smul_done, c * (JC + 1) + (m - 1))
                    for up in range(2):
                        for k in range(DC):
                            at = (up * JC + m) * P
                            last = nc.tensor.matmul(ps[:, 2 * (m % 2) + up, :], swug[:, k, at:at + P],
                                                    xT1[:, k, ds(c * (CT * P), CT * P)], start=(k == 0), stop=(k == DC - 1))
                    last.then_inc(sgu_done, 1)
                for k in range(DC):
                    last = nc.tensor.matmul(ps[:, 5, :], swug[:, k, 2 * JC * P:2 * J], xT1[:, k, ds(c * (CT * P), CT * P)],
                                            start=(k == 0), stop=(k == DC - 1))
                last.then_inc(sgu_done, 1)
                pe.wait_ge(ao_fetched, c + 1)
                wait_alone(pe, "pe", aoT_copied, START + c)
                for n in range(CT):
                    last = nc.tensor.transpose(ps[0:KD, 4, n * P:(n + 1) * P], aos[:, n, :], ident[:, :])
                last.then_inc(aoT_done, 1)
                pe.wait_ge(comb_step, START + c * CS)
                for n in range(CT):
                    to = ps[:, 6 + n // 2, (n % 2) * D:(n % 2 + 1) * D]
                    for m in range(JC + 1):
                        if n == 0 and m == JC - 1:
                            pe.wait_ge(smul_done, (c + 1) * (JC + 1))
                            pe.wait_ge(aoT_copied, START + c + 1)
                        elif n == 0 and m == 0:
                            pe.wait_ge(smul_done, c * (JC + 1) + (JC - 1))
                        last = nc.tensor.matmul(to, hTs[:, m, n * P:(n + 1) * P], swdn[:, m, :], start=(m == 0), stop=(m == JC))
                    last.then_inc(sdown_done, 1)

        def step_rows(s):
            return [32 * (2 * (s % 2) + k // UNIT) + UNIT * (s % STEPS // 2) + k % UNIT for k in range(STEP_ROWS)]

        @block.scalar
        def _(act):
            act.wait_ge(consts_loaded, CONSTS)
            with act.Fori(0, NB) as b:
                act.wait_ge(t1_ready, START + b + 1)
                act.wait_ge(qkv_ready, START + b)
                nc.scalar.activation(xT1s, ps_t1, ACT.Copy).then_inc(xT1s_ready, 1)
                nc.scalar.activation(xT1[:, :, ds(b * S, S)], ps_t1, ACT.Copy).then_inc(xT1_kept, 1)
                act.wait_ge(t2_ready, START + b + 1)
                for c in range(DC):
                    nc.scalar.activation(xn2T[:, c, :], ps_t2[:, c, :], ACT.Identity, scale=gamma[:, c:c + 1],
                                         bias=beta[:, c:c + 1]).then_inc(xn2T_ready, 1)
                act.wait_ge(h_ready, b + 1)
                nc.scalar.activation(hneg[:, ds(b * S, S)], ps_h, ACT.Copy, scale=-1.0).then_inc(h_saved, 1)
                nc.scalar.activation(hb[:, ds(b * S, S)], ps_h, ACT.Identity, bias=b1[:, 0:1]).then_inc(h_saved, 1)
            act.wait_ge(slots_zeroed, 16 * 5)
            act.wait_ge(kv_stored, START + 16 * NB)
            act.wait_ge(h_saved, START + 2 * NB)
            act.wait_ge(xT1_kept, START + NB)

            def relu1(b, s, first):
                if not (first and s < R1):
                    act.wait_ge(l2_done, b * BSTEPS + (s - R1 + 1))
                rows = step_rows(s)
                for k in range(dve_rows(s), STEP_ROWS):
                    at = b * S + ((s // STEPS) * P + rows[k])
                    last = nc.scalar.activation(r1[:, s % R1, k, :], hneg[:, ds(b * S, S)], ACT.Relu, bias=hb[:, ds(at, 1)])
                last.then_inc(r1_act, 1)

            def relu2(steps, s, wait_group):
                act.wait_ge(l2_done, steps)
                if wait_group is not None:
                    act.wait_ge(l3_done, wait_group)
                nc.scalar.activation(r2[:, s % R2, :].rearrange("p (u n) -> p u n", u=2), ps_l2(s), ACT.Relu, bias=b2[:, 0:1]).then_inc(r2_done, 1)

            def copy_sim(t, h, first):
                act.wait_ge(l3_done, t * GROUPS + GROUPS)
                if not first:
                    act.wait_ge(topk_step, t * TS)
                nc.scalar.activation(z0, ps_sim(h), ACT.Identity, bias=b3[:, 0:1]).then_inc(sim_copied, 1)

            def exp_scores(t):
                act.wait_ge(attn_step, t * AS + 3)
                nc.scalar.activation(sc, sc, ACT.Exp, scale=SCALE).then_inc(exp_ready, 1)

            def pair_batch(b, first):
                for s in range(BSTEPS):
                    h = s // STEPS
                    relu1(b, s, first)
                    if first and s == 8:
                        act.wait_ge(dlog_ready, 1)
                        nc.scalar.activation(edlog, dlog, ACT.Exp).then_inc(exp_routed, 1)
                    if s % STEPS == 3 and not (first and h == 0):
                        copy_sim(b * HALVES + (h - 1), 1 - h, first)
                    if not (first and s == 0):
                        relu2(b * BSTEPS + s, (s - 1) % BSTEPS, None if first and s - 1 < R2 else b * (BSTEPS // 2) + ((s - 1) // 2 - 1))
                    if s % STEPS == 10 and not first:
                        exp_scores(b * HALVES + (h - 2))

            pair_batch(0, True)
            with act.Fori(1, NB) as b:
                pair_batch(b, False)
            relu2(NB * BSTEPS, BSTEPS - 1, NB * (BSTEPS // 2) - 2)
            copy_sim(NT - 1, 1, False)

            act.wait_ge(l3_done, NT * GROUPS)

            def copy_xt(j, g):
                act.wait_ge(xt_done, j * GB + (g + 1))
                if g >= 2:
                    act.wait_ge(gu_done, j * GB + (g - 1))
                nc.scalar.activation(xTe[g % 2], ps_xt(g), ACT.Copy).then_inc(xt_copied, 1)

            def expert_pair(j, attended=None):
                copy_xt(j, 0)
                for g in range(GB):
                    if g < GB - 1:
                        copy_xt(j, g + 1)
                    act.wait_ge(gu_done, j * GB + (g + 1))
                    if g >= 2:
                        act.wait_ge(mul_done, j * GB + (g - 1))
                    nc.scalar.activation(sge[g % 2][0:IM, 0, :], ps_gate(g), ACT.Silu)
                    nc.scalar.activation(sge[g % 2][TAIL:2 * TAIL, 1, :], ps_tail(g)[0:TAIL], ACT.Silu).then_inc(silu_done, 1)
                    if g == 5 and attended is not None:
                        exp_scores(attended)

            for j in range(2):
                expert_pair(j, NT - 2 + j)
            with act.Fori(2, E // 2) as j:
                expert_pair(j)
            act.wait_ge(attn_step, AS * NT)

            with act.Fori(0, NCH) as c:
                for m in range(JC + 1):
                    act.wait_ge(sgu_done, c * (JC + 1) + (m + 1))
                    if m >= 2:
                        act.wait_ge(smul_done, c * (JC + 1) + (m - 1))
                    if m < JC:
                        nc.scalar.activation(sgs[m % 2], ps[:, 2 * (m % 2), :], ACT.Silu).then_inc(ssilu_done, 1)
                    else:
                        nc.scalar.activation(sgs[m % 2][KD:KD + TAIL], ps[0:TAIL, 5, :], ACT.Silu).then_inc(ssilu_done, 1)
                act.wait_ge(aoT_done, START + c + 1)
                act.wait_ge(sdown_done, START + c * CT)
                nc.scalar.activation(hTs[0:KD, JC, :], ps[0:KD, 4, :], ACT.Copy).then_inc(aoT_copied, 1)

        @block.vector
        def _(dve):
            def layernorm(b, r):
                at = START + b * LN + r * LN1

                def source(h):
                    return xn1[:, ds(b * HALVES + h, 1), :].rearrange("p o d -> p (o d)") if r == 0 else xn1s[:, h, :]

                dve.wait_ge(ln_step, at)
                for h in range(HALVES):
                    nc.vector.bn_stats(stats[:, r, h, :], source(h)).then_inc(ln_step, 1)
                for h in range(HALVES):
                    wait_alone(dve, "dve", ln_step, at + (HALVES + h))
                    nc.vector.bn_aggr(mv[:, r, h, :], stats[:, r, h, :]).then_inc(ln_step, 1)
                dve.wait_ge(ln_step, at + 2 * HALVES)
                nc.vector.tensor_scalar(veps[:, r, :], mv[:, r, :, 1], EPS, None, ALU.add).then_inc(ln_step, 1)

            def normalize(b, r):
                dve.wait_ge(rstd_ready, b * 2 + (r + 1))
                dve.wait_ge(t2_ready if r else t1_ready, START + b)
                for h in range(HALVES):
                    x_h = xn1[:, ds(b * HALVES + h, 1), :].rearrange("p o d -> p (o d)")
                    nc.vector.tensor_scalar((xn2s if r else xn1s)[:, h, :], xn1s[:, h, :] if r else x_h, mv[:, r, h, 0:1],
                                            rstd[:, r, h:h + 1], ALU.subtract, ALU.mult).then_inc(ln_step, 1)
                if r == 0:
                    for h in range(HALVES):
                        x_h = xn1[:, ds(b * HALVES + h, 1), :].rearrange("p o d -> p (o d)")
                        nc.vector.tensor_scalar(x_h, x_h, mv[:, r, h, 0:1], rstd[:, r, h:h + 1], ALU.subtract, ALU.mult)\
                            .then_inc(ln_step, 1)

            def save_projections(b):
                dve.wait_ge(qkv_ready, START + b + 1)
                nc.vector.tensor_tensor(qao[:, ds(b * HALVES, HALVES), :], ps_qkv[:, :, 0:KD],
                                        bqkv[:, 0:KD].unsqueeze(1).to_broadcast([P, HALVES, KD]), ALU.add).then_inc(qkv_saved, 1)
                nc.vector.tensor_copy(logits[:, ds(b * HALVES, HALVES), :], ps_logit).then_inc(qkv_saved, 1)

                dve.wait_ge(kv_stored, START + b * 16)
                nc.vector.tensor_tensor(kvs, ps_qkv[:, :, KD:3 * KD],
                                        bqkv[:, KD:3 * KD].unsqueeze(1).to_broadcast([P, HALVES, 2 * KD]), ALU.add)\
                    .then_inc(qkv_saved, 1)

            dve.wait_ge(x_first_loaded, 16)
            for r in range(2):
                layernorm(0, r)
                normalize(0, r)
            dve.wait_ge(x_rest_loaded, 48)
            dve.wait_ge(consts_loaded, CONSTS)
            with dve.Fori(1, NB) as b:
                for r in range(2):
                    layernorm(b, r)
                    normalize(b, r)
                save_projections(b - 1)
            save_projections(NB - 1)

            steps = [0]

            def link(ins):
                steps[0] += 1
                ins.then_inc(route_step, 1)
                dve.wait_ge(route_step, steps[0])

            def route_choose():
                for t in range(NT):
                    nc.vector.max(best[:, t, :], logits[:, t, :]).then_inc(route_step, 1)
                steps[0] = NT
                dve.wait_ge(route_step, NT)
                link(nc.vector.tensor_tensor(dlog.rearrange("p (t o) -> p t o", o=1), best[:, :, 1:2], best[:, :, 0:1], ALU.subtract))
                dve.sem_inc(dlog_ready, 1)
                for t in range(NT):
                    nc.vector.max_index(besti[:, t, :], best[:, t, :], logits[:, t, :]).then_inc(route_step, 1)
                steps[0] += NT
                dve.wait_ge(route_step, steps[0])
                link(nc.vector.tensor_copy(expert, besti[:, :, 0:2]))
                for k in range(2):
                    link(nc.vector.tensor_tensor(hot[k], iota8[:, :].unsqueeze(1).to_broadcast([P, NT, E]),
                                                 expert[:, :, k:k + 1].to_broadcast([P, NT, E]), ALU.is_equal))
                nc.vector.tensor_tensor(hots, hot[0], hot[1], ALU.add).then_inc(hot_ready, 1)

            def route_place():
                dve.wait_ge(exp_routed, 1)
                link(nc.vector.tensor_scalar(eden, edlog, 1.0, None, ALU.add))
                w0 = route_w[:, :, 0:1].rearrange("p t o -> p (t o)")
                w1 = route_w[:, :, 1:2].rearrange("p t o -> p (t o)")
                link(nc.vector.reciprocal(w0, eden))
                link(nc.vector.tensor_tensor(w1, w0, edlog, ALU.mult))
                dve.wait_ge(counts_ready, 1)
                for e in range(E):
                    link(nc.vector.tensor_tensor_scan(filled[:, :, e], ones[:, 0:NT], ps_count[:, :, e], 0.0, ALU.mult, ALU.add))
                link(nc.vector.tensor_tensor(base, filled, ps_count, ALU.subtract))
                link(nc.vector.tensor_tensor(base, base, ps_before, ALU.add))
                for k in range(2):
                    link(nc.vector.tensor_tensor(hotpos[k], hot[k], base, ALU.mult))
                    link(nc.vector.tensor_reduce(pos[:, :, k], hotpos[k], AX, ALU.add))
                link(nc.vector.tensor_scalar(posc, pos, float(CAP - 1), None, ALU.min))
                link(nc.vector.tensor_scalar(valid, pos, float(CAP), None, ALU.is_lt))
                link(nc.vector.tensor_scalar(over, pos, float(CAP), float(2 * SLOTS), ALU.is_ge, ALU.mult))
                link(nc.vector.scalar_tensor_tensor(slotf, expert, float(CAP), posc, ALU.mult, ALU.add))
                link(nc.vector.tensor_copy(slot_get[:, :, :], slotf))
                link(nc.vector.tensor_tensor(slot_put[:, :].rearrange("p (t k) -> p t k", k=2), slotf, over, ALU.add))
                link(nc.vector.tensor_tensor(route_w[:, :, :], route_w[:, :, :], valid, ALU.mult))
                dve.sem_inc(route_done, 1)

            dve.wait_ge(made, 10)
            dve.wait_ge(qkv_saved, START + 3 * NB)
            dve.wait_ge(slots_zeroed, 16 * 5)
            dve.wait_ge(kv_stored, START + 16 * NB)
            dve.wait_ge(h_saved, START + 2 * NB)
            dve.wait_ge(xT1_kept, START + NB)

            def relu1_begin(b, s, first):
                if not (first and s < R1):
                    dve.wait_ge(l2_done, b * BSTEPS + (s - R1 + 1))

            def relu1_rows(b, s, ks):
                rows = step_rows(s)
                for k in ks:
                    at = b * S + ((s // STEPS) * P + rows[k])
                    row = nc.vector.tensor_scalar(r1[:, s % R1, k, :], hneg[:, ds(b * S, S)], hb[:, ds(at, 1)], 0.0, ALU.add, ALU.max)
                    if k == dve_rows(s) - 1:
                        row.then_inc(r1_dve, 1)

            zs = [z0, z1, z0, z1]


            def topk_max(t, r):
                if r == 0:
                    wait_alone(dve, "dve", diag_cleared, t + 1)
                else:
                    wait_alone(dve, "dve", topk_step, t * TS + 3 * r)
                nc.vector.max(top8[:, r, :], zs[r]).then_inc(topk_step, 1)

            def topk_find(t, r):
                wait_alone(dve, "dve", topk_step, t * TS + (3 * r + 1))
                if r < ROUNDS - 1:
                    nc.vector.match_replace(zs[r + 1], top8[:, r, :], zs[r], LOWEST).then_inc(topk_step, 1)
                nc.vector.max_index(idx8[:, r, :], top8[:, r, :], zs[r]).then_inc(topk_step, 1)

            def topk_rows(t, h, b, r):
                dve.wait_ge(topk_step, t * TS + min(3 * r + 3, TS))
                nc.vector.tensor_scalar(gidx[:, h, 8 * r:8 * r + 8], idx8[:, r, :], batch_row[:, ds(b, 1)], None, ALU.add)\
                    .then_inc(idx_ready, 1)

            def attention(t, h, a):
                n = t * AS
                if a == 0:
                    dve.wait_ge(prod_ready, t + 1)
                    nc.vector.tensor_tensor(sc.rearrange("p r h -> p (r h)"),
                                            prod.rearrange("p r (h d) -> p (r h) d", d=2)[:, :, 0],
                                            prod.rearrange("p r (h d) -> p (r h) d", d=2)[:, :, 1], ALU.add).then_inc(attn_step, 1)
                elif a == 1:
                    dve.wait_ge(attn_step, n + 1)
                    nc.vector.tensor_reduce(smax[:, :], sc.rearrange("p r h -> p h r"), AX, ALU.max).then_inc(attn_step, 1)
                elif a == 2:
                    dve.wait_ge(attn_step, n + 2)
                    nc.vector.tensor_tensor(sc, sc, smax[:, :].unsqueeze(1).to_broadcast([P, TOPK, HEADS]), ALU.subtract)\
                        .then_inc(attn_step, 1)
                elif a == 3:
                    dve.wait_ge(exp_ready, t + 1)
                    nc.vector.tensor_reduce(sden[:, :], sc.rearrange("p r h -> p h r"), AX, ALU.add).then_inc(attn_step, 1)
                elif a == 4:
                    dve.wait_ge(attn_step, n + 4)
                    nc.vector.reciprocal(srec[:, :], sden[:, :]).then_inc(attn_step, 1)
                elif a == 5:
                    nc.vector.tensor_tensor(pv.rearrange("p r (h d) -> p r h d", d=2),
                                            kvg[:, h, :, KD:2 * KD].rearrange("p r (h d) -> p r h d", d=2),
                                            sc.unsqueeze(3).to_broadcast([P, TOPK, HEADS, 2]), ALU.mult).then_inc(attn_step, 1)
                elif a == 6:
                    dve.wait_ge(attn_step, n + 6)
                    nc.vector.tensor_reduce(aosum[:, :], pv.rearrange("p r k -> p k r"), AX, ALU.add).then_inc(attn_step, 1)
                elif a == 7:
                    dve.wait_ge(attn_step, n + 7)
                    nc.vector.tensor_tensor(qao[:, ds(t, 1), :].rearrange("p o (h d) -> p (o h) d", d=2),
                                            aosum[:, :].rearrange("p (h d) -> p h d", d=2),
                                            srec[:, :].unsqueeze(2).to_broadcast([P, HEADS, 2]), ALU.mult).then_inc(attn_step, 1)

            AT = {7: (0,), 8: (1,), 9: (2,), 13: (3,), 14: (4, 5), 15: (6, 7)}
            TOP = 6

            def pair_batch(b, first):
                for s in range(BSTEPS):
                    h, s16 = s // STEPS, s % STEPS
                    r = s16 - TOP
                    topk = 0 <= r <= ROUNDS and not (first and h == 0)
                    prev, prev_b = b * HALVES + (h - 1), b if h else b - 1
                    n = dve_rows(s)
                    if first and s == 4:
                        route_choose()
                    if first and s == 10:
                        route_place()
                    relu1_begin(b, s, first)
                    relu1_rows(b, s, range(2))
                    if topk and r < ROUNDS:
                        topk_max(prev, r)
                    if topk and r:
                        topk_rows(prev, 1 - h, prev_b, r - 1)
                    for a in () if first else AT.get(s16, ()):
                        attention(b * HALVES + (h - 2), h, a)
                    relu1_rows(b, s, range(2, n))
                    if topk and r < ROUNDS:
                        topk_find(prev, r)

            pair_batch(0, True)
            with dve.Fori(1, NB) as b:
                pair_batch(b, False)
            for r in range(ROUNDS):
                topk_max(NT - 1, r)
                topk_find(NT - 1, r)
                topk_rows(NT - 1, 1, NB - 1, r)
            dve.wait_ge(l3_done, NT * GROUPS)

            def gate_times_up(j, g):
                dve.wait_ge(silu_done, j * GB + (g + 1))
                if g >= 2:
                    dve.wait_ge(down_done, j * GB + (g - 1))
                nc.vector.tensor_tensor(hTe[g % 2][0:IM, 0, :], sge[g % 2][0:IM, 0, :], ps_up(g), ALU.mult)
                nc.vector.tensor_tensor(hTe[g % 2][TAIL:2 * TAIL, 1, :], sge[g % 2][TAIL:2 * TAIL, 1, :],
                                        ps_tail(g)[TAIL:2 * TAIL], ALU.mult).then_inc(mul_done, 1)

            def copy_down(j, g):
                i = g // GPE
                dve.wait_ge(down_done, j * GB + (g + 1))
                if g % GPE == 0:
                    dve.wait_ge(y_stored[i], START + j * 16)
                n0 = 2 * (g % GPE)
                nc.vector.tensor_copy(oute[i][:, n0:n0 + 2, :], ps_down(g)).then_inc(down_copied, 1)

            EAT = {2: (0,), 3: (1,), 4: (2,), 6: (3, 4), 7: (5,), 8: (6,), 9: (7,)}

            def expert_pair(j, attended=None):
                for g in range(GB):
                    gate_times_up(j, g)
                    if g:
                        copy_down(j, g - 1)
                    for a in () if attended is None else EAT.get(g, ()):
                        attention(attended, attended % 2, a)
                copy_down(j, GB - 1)

            for j in range(2):
                expert_pair(j, NT - 2 + j)
            with dve.Fori(2, E // 2) as j:
                expert_pair(j)

            with dve.Fori(0, NCH) as c:
                dve.wait_ge(sdown_done, START + c * CT)
                for m in range(JC + 1):
                    dve.wait_ge(ssilu_done, c * (JC + 1) + (m + 1))
                    rows, bank = (slice(0, P), 2 * (m % 2) + 1) if m < JC else (slice(KD, KD + TAIL), 5)
                    nc.vector.tensor_tensor(hTs[rows, m, :], sgs[m % 2][rows], ps[rows, bank, :], ALU.mult)\
                        .then_inc(smul_done, 1)
                dve.wait_ge(ys_gathered, c * (16 * 2 * CT) + 16 * 2 * CT)
                dve.wait_ge(out_stored, START + c * 16)
                for n in range(CT):
                    dve.wait_ge(sdown_done, START + c * CT + (n // 2 * 2 + 2))
                    nc.vector.scalar_tensor_tensor(fin[:, n, :], ys[:, n, 0, :], route_w[:, ds(c * CT + n, 1), 0:1].rearrange("p a b -> p (a b)"),
                                                   ps[:, 6 + n // 2, (n % 2) * D:(n % 2 + 1) * D], ALU.mult, ALU.add)\
                        .then_inc(comb_step, 1)
                for n in range(CT):
                    dve.wait_ge(comb_step, START + c * CS + (n + 1))
                    nc.vector.scalar_tensor_tensor(fin[:, n, :], ys[:, n, 1, :], route_w[:, ds(c * CT + n, 1), 1:2].rearrange("p a b -> p (a b)"),
                                                   fin[:, n, :], ALU.mult, ALU.add).then_inc(comb_step, 1)
                dve.wait_ge(resid_ready, c * 2 + 2)
                for n in range(CT):
                    dve.wait_ge(comb_step, START + c * CS + (CT + n + 1))
                    nc.vector.tensor_tensor(fin[:, n, :], fin[:, n, :], resid[:, n, :], ALU.add).then_inc(comb_step, 1)


_PRE = "L0_attn_"
_INS = [("L0_attn_x", False), ("L0_attn_gamma", False), ("L0_attn_beta", False), ("L0_attn_W1", True), ("L0_attn_b1", False),
        ("L0_attn_W2", True), ("L0_attn_b2", False), ("L0_attn_W3", False), ("L0_attn_b3", False), ("L0_attn_Wqkv", True),
        ("L0_attn_bqkv", False), ("L0_attn_Wout", True), ("L0_attn_bout", False), ("L0_ffn_router", False),
        ("L0_ffn_w_up_gate", False), ("L0_ffn_w_down", False), ("L0_ffn_shared_w_up_gate", False),
        ("L0_ffn_shared_w_down", False)]
_OUTS = [((16, 256, 256), "float32")]


def kernel(**inputs):
    import numpy as _np
    import concourse.bacc as _bacc
    from concourse import mybir as _mybir
    from concourse.bass_utils import run_bass_kernel_spmd as _run

    nc = _bacc.Bacc("TRN2", target_bir_lowering=False, num_devices=1)
    arrays, args = {}, []
    for name, transposed in _INS:
        a = _np.asarray(inputs[name])
        if transposed:
            a = a.T
        elif name.endswith("up_gate"):
            g = a.reshape(a.shape[:-1] + (2, a.shape[-1] // 2))
            main, tail = g[..., :-64], g[..., -64:]
            a = _np.concatenate([p.reshape(a.shape[:-1] + (-1,)) for p in (main, tail)], axis=-1)
        a = _np.ascontiguousarray(a)
        arrays[f"in_{name}_dram"] = a
        args.append(nc.dram_tensor(f"in_{name}_dram", a.shape, _mybir.dt.from_np(a.dtype), kind="ExternalInput").ap())
    for i, (shape, dtype) in enumerate(_OUTS):
        dt = _mybir.dt.from_np(_np.dtype(dtype))
        args.append(nc.dram_tensor(f"out_{i}_dram", shape, dt, kind="ExternalOutput").ap())
    lsn_attention_moe_block(nc, *args)
    r = _run(nc, [arrays], core_ids=[0])
    got = tuple(r.results[0][f"out_{i}_dram"] for i in range(len(_OUTS)))
    return got[0]
```

```python
import concourse.bass as bass
from concourse import mybir
from contextlib import ExitStack


def lsn_attention_moe_block(
    nc: bass.Bass,
    x_d: bass.AP,
    gamma_d: bass.AP,
    beta_d: bass.AP,
    w1t_d: bass.AP,
    b1_d: bass.AP,
    w2t_d: bass.AP,
    b2_d: bass.AP,
    w3_d: bass.AP,
    b3_d: bass.AP,
    wqkvt_d: bass.AP,
    bqkv_d: bass.AP,
    woutt_d: bass.AP,
    bout_d: bass.AP,
    router_d: bass.AP,
    wug_d: bass.AP,
    wdn_d: bass.AP,
    swug_d: bass.AP,
    swdn_d: bass.AP,
    out_d: bass.AP,
):
    f32 = mybir.dt.float32
    u32 = mybir.dt.uint32
    f32r = mybir.dt.float32r
    ALU = mybir.AluOpType
    ACT = mybir.ActivationFunctionType
    AX = mybir.AxisListType.X
    ds = bass.ds

    P = 128
    NB, S, D = x_d.shape
    DC = D // P
    NT = NB * S // P
    HALVES = S // P
    F1, G2 = w2t_d.shape
    KD = woutt_d.shape[0]
    HEADS, HD = 32, KD // 32
    TOPK = max(1, int(S * 0.1))
    ROUNDS = (TOPK + 7) // 8
    EPS = 1e-5
    SCALE = float(HD) ** -0.5
    E = router_d.shape[1]
    TOKENS = NB * S
    CAP = -(-TOKENS * 2 * 5 // (E * 4))
    SLOTS = E * CAP
    I = wdn_d.shape[1]
    TAIL = 64
    IM = I - TAIL
    J = swdn_d.shape[0]
    JC = (J - TAIL) // P
    LOWEST = -3.0e38

    UNIT = 4
    STEP_ROWS = 2 * UNIT
    STEPS = P // STEP_ROWS
    BSTEPS = HALVES * STEPS
    R1 = 4
    R2 = 4

    NPE = CAP // P
    GPE = NPE // 2
    GB = 2 * GPE
    CT = 4
    NCH = NT // CT

    x_t = x_d.rearrange("b (h p) d -> p (b h) d", p=P)
    out_t = out_d.rearrange("b (h p) d -> p (b h) d", p=P)
    kv_dram = nc.dram_tensor("kv_rows", (TOKENS, 2 * KD), f32, kind="Internal").ap()
    slot_dram = nc.dram_tensor("slot_inputs", (SLOTS, D), f32, kind="Internal").ap()
    yslot_dram = nc.dram_tensor("slot_outputs", (SLOTS, D), f32, kind="Internal").ap()

    ctx = ExitStack()
    with ctx:
        def sb(name, shape, dt=f32):
            return ctx.enter_context(nc.sbuf_tensor(name, shape, dt))

        def sem(name):
            return ctx.enter_context(nc.semaphore(name))

        xn1 = sb("xn1", [P, NT, D])
        xT1 = sb("xT1", [P, DC, TOKENS])
        qao = sb("qao", [P, NT, KD])
        w1t = sb("w1t", [P, DC, F1])
        wqkvt = sb("wqkvt", [P, DC, 3 * KD])
        router = sb("router", [P, DC, E])
        w2t = sb("w2t", [F1, G2])
        w3win = sb("w3win", [2 * G2, 64])
        gamma = sb("gamma", [P, DC])
        beta = sb("beta", [P, DC])
        b1 = sb("b1", [F1, 1])
        b2 = sb("b2", [2 * G2, 1])
        b3 = sb("b3", [P, 1])
        bqkv = sb("bqkv", [P, 3 * KD])
        bout = sb("bout", [P, D])
        ident = sb("ident", [P, P])
        earlier = sb("earlier", [P, P])
        ones = sb("ones", [P, P])
        iota8 = sb("iota8", [P, E])
        batch_row = sb("batch_row", [P, NB])
        route_w = sb("route_w", [P, NT, 2])
        slot_get = sb("slot_get", [P, NT, 2], u32)
        slot_put = sb("slot_put", [P, NT * 2], u32)

        ARENA = 31392
        arena = sb("arena", [P, ARENA])
        arena_at = nc.sbuf_base - 4 * ARENA
        taken = [0]

        def halves(name, n, *dims):
            pair = []
            for half in ("high", "low"):
                pair.append(nc.alloc_sbuf_tensor_at(f"{name}_{half}", [P, *dims], f32r, offset=arena_at + 4 * taken[0]))
                part(n)
            return pair

        def part(n, *dims):
            at = taken[0]
            taken[0] = at + n
            assert taken[0] <= ARENA
            view = arena[:, at:at + n]
            if len(dims) == 1:
                return view.rearrange("p (a b) -> p a b", a=dims[0])
            if len(dims) == 2:
                return view.rearrange("p (a b c) -> p a b c", a=dims[0], b=dims[1])
            return view

        hneg = part(TOKENS)
        hb = part(TOKENS)
        rows_base = taken[0]
        r1 = part(R1 * STEP_ROWS * S, R1, STEP_ROWS)
        r2 = part(R2 * 2 * 512, R2)
        attn_base = taken[0]
        kvg = part(2 * TOPK * 2 * KD, 2, TOPK)
        prod = part(TOPK * KD, TOPK)
        sc = part(TOPK * HEADS, TOPK)
        pv = part(TOPK * KD, TOPK)
        z0 = part(S)
        z1 = part(S)
        pair_end = taken[0]
        top8 = sb("top8", [P, ROUNDS, 8])
        idx8 = sb("idx8", [P, ROUNDS, 8], u32)
        gidx = sb("gidx", [P, 2, ROUNDS * 8], u32)
        smax = sb("smax", [P, HEADS])
        sden = sb("sden", [P, HEADS])
        srec = sb("srec", [P, HEADS])
        aosum = sb("aosum", [P, KD])

        taken[0] = rows_base
        xn1s = part(HALVES * D, HALVES)
        xn2s = part(HALVES * D, HALVES)
        xT1s = part(DC * S, DC)
        xn2T = part(DC * S, DC)
        stats = part(2 * HALVES * 6, 2, HALVES)
        mv = part(2 * HALVES * 2, 2, HALVES)
        veps = part(2 * HALVES, 2)
        rstd = part(2 * HALVES, 2)
        neg_half = part(HALVES)
        taken[0] = rows_base + R1 * STEP_ROWS * S
        kvs = part(HALVES * 2 * KD, HALVES)
        zeros = part(SLOTS // P * D // NB)
        assert taken[0] <= attn_base
        taken[0] = attn_base + TOPK * 2 * KD
        logits = part(NT * E, NT)
        best = part(NT * E, NT)
        besti = part(NT * E, NT).bitcast(u32)
        expert = part(NT * 2, NT)
        dlog = part(NT)
        edlog = part(NT)
        eden = part(NT)
        hot = [part(NT * E, NT) for _ in range(2)]
        hots = part(NT * E, NT)
        filled = part(NT * E, NT)
        base = part(NT * E, NT)
        hotpos = [part(NT * E, NT) for _ in range(2)]
        pos = part(NT * 2, NT)
        posc = part(NT * 2, NT)
        slotf = part(NT * 2, NT)
        over = part(NT * 2, NT)
        valid = part(NT * 2, NT)
        assert taken[0] <= attn_base + 2 * TOPK * 2 * KD

        taken[0] = 0
        xe = [part(2 * D, 2) for _ in range(GPE)]
        wug = part(DC * 2 * I, DC)
        wdn = part(2 * D, 2)
        wug_r, wdn_r = [], []
        for i in range(2):
            wug_r.append(halves(f"wug{i}", DC * 2 * I, DC, 2 * I))
            wdn_r.append(halves(f"wdn{i}", 2 * D, 2, D))
            if i == 0:
                assert taken[0] <= 2 * TOKENS
        xTe_r = [halves(f"xTe{i}", DC * 256, DC, 256) for i in range(2)]
        sge = [part(2 * 256, 2) for _ in range(2)]
        hTe_r = [halves(f"hTe{i}", 2 * 256, 2, 256) for i in range(2)]
        oute = [part(2 * D, 2) for _ in range(2)]
        experts_end = taken[0]
        swug = part(DC * 2 * J, DC)
        swdn = part((JC + 1) * D, JC + 1)
        assert taken[0] <= attn_base
        taken[0] = attn_base
        swug_r = halves("swug", DC * 2 * J, DC, 2 * J)
        swdn_r = halves("swdn", (JC + 1) * D, JC + 1, D)
        xT_r = halves("xT", DC * 512, DC, 512)
        taken[0] = 0
        resid = part(CT * D, CT)
        fin = part(CT * D, CT)
        ys = part(CT * 2 * D, CT, 2)
        sgs = [part(512) for _ in range(2)]
        hTs_r = halves("hTs", (JC + 1) * 512, JC + 1, 512)
        aos = part(CT * KD, CT)
        assert taken[0] <= experts_end
        ysidx = sb("ysidx", [P, CT, 2], u32)
        xstage = sb("xstage", [P, HALVES, D])
        istage = sb("istage", [P, HALVES * 2], u32)

        ps = ctx.enter_context(nc.psum_tensor("ps", [P, 8, 512], f32))

        ps_t1 = ps[:, 0, :].rearrange("p (c s) -> p c s", c=DC)
        ps_t2 = ps[:, 1, :].rearrange("p (c s) -> p c s", c=DC)
        ps_h = ps[:, 2, 0:S]
        ps_qkv = ps[:, 3, :].rearrange("p (h n) -> p h n", h=HALVES)
        ps_logit = ps[:, 4, 0:HALVES * E].rearrange("p (h n) -> p h n", h=HALVES)
        ps_before = ps[:, 7, 0:NT * E].rearrange("p (t e) -> p t e", e=E)
        ps_count = ps[:, 7, NT * E:2 * NT * E].rearrange("p (t e) -> p t e", e=E)

        PS2 = 3

        def ps_l2(s):
            return ps[:, 2 * (s % PS2):2 * (s % PS2) + 2, :]

        def ps2_before(s):
            if s >= PS2:
                return s - PS2
            return max(x for x in range(BSTEPS) if x % PS2 == s) - BSTEPS

        def ps_sim(h):
            return ps[:, 6 + h, 0:S]

        def ps_xt(g):
            return ps[:, 6 + g % 2, :].rearrange("p (c n) -> p c n", c=DC)

        def ps_gate(g):
            return ps[0:IM, 2 * (g % 2), 0:256]

        def ps_up(g):
            return ps[0:IM, 2 * (g % 2) + 1, 0:256]

        def ps_tail(g):
            return ps[:, 2 * (g % 2), 256:512]

        def ps_down(g):
            return ps[:, 4 + g % 2, :].rearrange("p (n d) -> p n d", n=2)

        consts_loaded = sem("consts_loaded")
        x_loaded = sem("x_loaded")
        made = sem("made")
        ln_step = [sem(f"ln{r + 1}_step") for r in range(2)]
        rstd_ready = [sem(f"rstd{r + 1}_ready") for r in range(2)]
        logits_ready = sem("logits_ready")
        logits_saved = sem("logits_saved")
        t1_ready = sem("t1_ready")
        t2_ready = sem("t2_ready")
        xT1s_ready = sem("xT1s_ready")
        xn2T_ready = sem("xn2T_ready")
        h_ready = sem("h_ready")
        h_saved = sem("h_saved")
        qkv_ready = sem("qkv_ready")
        qkv_saved = sem("qkv_saved")
        kv_stored = sem("kv_stored")
        staged = sem("staged")
        xT1_kept = sem("xT1_kept")
        slots_zeroed = sem("slots_zeroed")
        route_step = sem("route_step")
        hot_ready = sem("hot_ready")
        dlog_ready = sem("dlog_ready")
        exp_routed = sem("exp_routed")
        counts_ready = sem("counts_ready")
        route_done = sem("route_done")
        scattered = sem("scattered")

        r1_dve = sem("r1_dve")
        r1_act = sem("r1_act")
        l2_done = sem("l2_done")
        r2_done = sem("r2_done")
        l3_done = sem("l3_done")
        sim_copied = sem("sim_copied")
        diag_cleared = sem("diag_cleared")
        topk_step = sem("topk_step")
        idx_ready = sem("idx_ready")
        gathered = sem("gathered")
        prod_ready = sem("prod_ready")
        attn_step = sem("attn_step")
        exp_ready = sem("exp_ready")

        xe_loaded = [sem(f"xe_loaded{i}") for i in range(GPE)]
        we_loaded = sem("we_loaded")
        we_high = sem("we_high")
        we_low = sem("we_low")
        xt_done = sem("xt_done")
        xt_high = sem("xt_high")
        xt_low = sem("xt_low")
        gu_done = sem("gu_done")
        silu_done = sem("silu_done")
        mul_done = sem("mul_done")
        h_high = sem("h_high")
        h_low = sem("h_low")
        down_done = sem("down_done")
        down_copied = sem("down_copied")
        y_stored = [sem(f"y_stored{i}") for i in range(2)]

        shared_loaded = sem("shared_loaded")
        sgu_done = sem("sgu_done")
        ssilu_done = sem("ssilu_done")
        smul_done = sem("smul_done")
        shigh_done = sem("shigh_done")
        slow_done = sem("slow_done")
        shared_high = sem("shared_high")
        shared_split = sem("shared_split")
        xT_split = sem("xT_split")
        aoT_high = sem("aoT_high")
        aoT_low = sem("aoT_low")
        ao_fetched = sem("ao_fetched")
        aoT_done = sem("aoT_done")
        sdown_done = sem("sdown_done")
        ysidx_ready = sem("ysidx_ready")
        ys_gathered = sem("ys_gathered")
        resid_loaded = sem("resid_loaded")
        resid_ready = sem("resid_ready")
        comb_step = sem("comb_step")
        out_stored = sem("out_stored")

        START = 1
        started = [*ln_step, logits_ready, logits_saved, t1_ready, t2_ready, xT1s_ready, xn2T_ready, h_saved, qkv_ready, qkv_saved, kv_stored, 
                   xT1_kept, comb_step, aoT_done, aoT_low, sgu_done, sdown_done, out_stored]

        N_CONST = 12 + 2 * DC
        CONSTS = 16 * N_CONST
        LN = [3 * HALVES + 2, 3 * HALVES + 1]
        TS = 3 * ROUNDS - 1
        AS = 8
        CS = 3 * CT

        GROUPS = STEPS // 2

        def dve_rows(s):
            return 6 if s % STEPS in (0, 1, 2, 3, 4, 10, 11, 15) else 5

        passed = {name: sem(f"{name}_passed") for name in ("dve", "pe", "pool")}

        def wait_alone(eng, name, what, value):
            eng.wait_ge(what, value)
            eng.sem_inc(passed[name], 1)

        WEIGHTS_AT = {(0, 2): 1, (0, 8): 2, (1, 3): 3}

        def expert_weights(i):
            return [(w, high, low) for w, high, low in (
                (wug, *(h[:, :, :] for h in wug_r[i])),
                (wdn[0:IM, 0, :], *(h[0:IM, 0, :] for h in wdn_r[i])),
                (wdn[TAIL:2 * TAIL, 1, :], *(h[TAIL:2 * TAIL, 1, :] for h in wdn_r[i])))]

        def expert_activations(g):
            return [(rows, sge[g % 2][rows, m, :], *(h[rows, m, :] for h in hTe_r[g % 2]))
                    for m, rows in enumerate((slice(0, IM), slice(TAIL, 2 * TAIL)))]

        block = ctx.enter_context(nc.Block())

        @block.sync
        def _(sp):
            def load_x(b):
                sp.dma_start(xn1[:, ds(b * HALVES, HALVES), :], x_t[:, ds(b * HALVES, HALVES), :]).then_inc(x_loaded, 16)

            load_x(0)
            for s in started:
                sp.sem_inc(s, START)
            for dst, src in (
                (w1t[:, :, :], w1t_d.rearrange("(c p) f -> p c f", p=P)),
                (wqkvt[:, :, :], wqkvt_d.rearrange("(c p) f -> p c f", p=P)),
                (router[:, :, :], router_d.rearrange("(c p) f -> p c f", p=P)),
                *((to[:, c:c + 1], src[c * P:(c + 1) * P].rearrange("(p o) -> p o", o=1))
                  for to, src in ((gamma, gamma_d), (beta, beta_d)) for c in range(DC)),
                (b1[:, :], b1_d.rearrange("(p o) -> p o", o=1)),
                (bqkv[:, :], bqkv_d.partition_broadcast(P)),
                (w2t[:, :], w2t_d),
                (b2[0:G2, :], b2_d.rearrange("(p o) -> p o", o=1)),
                (b2[G2:2 * G2, :], b2_d.rearrange("(p o) -> p o", o=1)),
                (b3[:, :], b3_d.partition_broadcast(P)),
                (bout[:, :], bout_d.partition_broadcast(P)),
            ):
                sp.dma_start(dst, src).then_inc(consts_loaded, 16)
            sp.wait_ge(made, 1)
            sp.dma_start(w3win[0:G2, 32:33], w3_d.rearrange("o g -> g o")).then_inc(consts_loaded, 16)
            sp.dma_start(w3win[G2:2 * G2, 34:35], w3_d.rearrange("o g -> g o")).then_inc(consts_loaded, 16)
            AHEAD = 4
            for b in range(1, AHEAD):
                sp.wait_ge(x_loaded, 16 * b)
                load_x(b)
            sp.wait_ge(made, 2)
            zv = slot_dram.rearrange("(k p n) d -> p k (n d)", k=NB, p=P)

            def store_batch(b):
                sp.dma_start(zv[:, ds(b, 1), :].rearrange("p k n -> p (k n)"), zeros).then_inc(slots_zeroed, 16)
                sp.wait_ge(qkv_saved, START + b * 2 + 2)
                sp.dma_start(kv_dram[ds(b * S, S), :].rearrange("(h p) n -> p h n", p=P), kvs)\
                  .then_inc(kv_stored, 16)

            with sp.Fori(0, NB - AHEAD) as b:
                sp.wait_ge(x_loaded, b * 16 + 16 * AHEAD)
                load_x(b + AHEAD)
                store_batch(b)
            with sp.Fori(NB - AHEAD, NB) as b:
                store_batch(b)

            sp.wait_ge(route_done, 1)
            sp.wait_ge(ln_step[0], START + NB * LN[0])

            def stage(b):
                sp.dma_start(xstage[:, :, :], xn1[:, ds(b * HALVES, HALVES), :]).then_inc(staged, 16)
                sp.dma_start(istage[:, :], slot_put[:, ds(b * (HALVES * 2), HALVES * 2)]).then_inc(staged, 16)

            stage(0)
            with sp.Fori(1, NB) as b:
                sp.wait_ge(scattered, b * (16 * 2 * HALVES))
                stage(b)

            sp.wait_ge(r1_dve, NB * BSTEPS)
            sp.wait_ge(r1_act, NB * BSTEPS)

            def expert_rows(dram, j, g):
                return dram[ds((j * 2 + g // GPE) * CAP, CAP), :].rearrange("(p n) d -> p n d", p=P)[:, 2 * (g % GPE):2 * (g % GPE) + 2, :]

            def load_weights(e):
                sp.dma_start(wug, wug_d[ds(e, 1), :, :].rearrange("o (c p) m -> p (o c) m", p=P)).then_inc(we_loaded, 16)
                sp.dma_start(wdn[0:IM, 0, :], wdn_d[ds(e, 1), 0:IM, :].rearrange("o p d -> p (o d)")).then_inc(we_loaded, 16)
                sp.dma_start(wdn[TAIL:2 * TAIL, 1, :], wdn_d[ds(e, 1), IM:I, :].rearrange("o p d -> p (o d)"))\
                  .then_inc(we_loaded, 16)

            def load_slots(j, g):
                sp.dma_start(xe[g % GPE], expert_rows(slot_dram, j, g)).then_inc(xe_loaded[g % GPE], 16)

            def store_group(j, g):
                sp.wait_ge(down_copied, j * GB + (g + 1))
                sp.dma_start(expert_rows(yslot_dram, j, g), oute[g % 2]).then_inc(y_stored[g % 2], 16)

            def expert_pair(j, first, last):
                for g in range(GB):
                    if not (last and g + GPE >= GB):
                        sp.wait_ge(xt_done, j * GB + (g + 1))
                        load_slots(j, g + GPE)
                    if not (first and g < 2):
                        store_group(j, g - 2)
                    if g % GPE == 1 and not (last and g > GPE):
                        sp.wait_ge(we_low, j * 6 + (g // GPE + 1) * 3)
                        load_weights(j * 2 + (g // GPE + 1))

            load_weights(0)
            sp.wait_ge(scattered, 16 * 2 * NT)
            for g in range(GPE):
                load_slots(0, g)
            sp.wait_ge(l3_done, NT * GROUPS)
            sp.dma_start(swug, swug_d.rearrange("(c p) m -> p c m", p=P)).then_inc(shared_loaded, 16)
            sp.dma_start(swdn[:, 0:JC, :], swdn_d[0:JC * P, :].rearrange("(c p) d -> p c d", p=P))\
              .then_inc(shared_loaded, 16)
            sp.dma_start(swdn[0:KD, JC, :], woutt_d).then_inc(shared_loaded, 16)
            sp.dma_start(swdn[KD:KD + TAIL, JC, :], swdn_d[JC * P:J, :]).then_inc(shared_loaded, 16)
            expert_pair(0, True, False)
            with sp.Fori(1, E // 2 - 1) as j:
                expert_pair(j, False, False)
            expert_pair(E // 2 - 1, False, True)
            for g in (GB - 2, GB - 1):
                store_group(E // 2 - 1, g)

            sp.wait_ge(xt_done, GB * (E // 2))

            def load_resid(c):
                sp.wait_ge(comb_step, START + c * CS)
                sp.dma_start(resid, x_t[:, ds(c * CT, CT), :]).then_inc(resid_loaded, 16)

            load_resid(0)
            with sp.Fori(0, NCH - 1) as c:
                load_resid(c + 1)
                sp.dma_start(out_t[:, ds(c * CT, CT), :], fin).then_inc(out_stored, 16)
            sp.wait_ge(comb_step, START + NCH * CS)
            sp.dma_start(out_t[:, (NCH - 1) * CT:NCH * CT, :], fin).then_inc(out_stored, 16)
            sp.wait_ge(out_stored, START + 16 * NCH)

        @block.gpsimd
        def _(pool):
            nc.gpsimd.memset(w3win[:, :], 0.0).then_inc(made, 1)
            nc.gpsimd.memset(zeros, 0.0).then_inc(made, 1)
            nc.gpsimd.memset(ident[:, :], 0.0).then_inc(made, 1)
            nc.gpsimd.memset(earlier[:, :], 1.0).then_inc(made, 1)
            nc.gpsimd.memset(ones[:, :], 1.0).then_inc(made, 1)
            nc.gpsimd.memset(neg_half, -0.5).then_inc(made, 1)
            pool.wait_ge(made, 6)
            nc.gpsimd.affine_select(out=ident[:, :], in_=ident[:, :], compare_op=ALU.not_equal, fill=1.0, base=0,
                                    pattern=[[-1, P]], channel_multiplier=1).then_inc(made, 1)
            nc.gpsimd.affine_select(out=earlier[:, :], in_=earlier[:, :], compare_op=ALU.is_gt, fill=0.0, base=0,
                                    pattern=[[1, P]], channel_multiplier=-1).then_inc(made, 1)
            nc.gpsimd.iota(iota8[:, :], pattern=[[1, E]], base=0, channel_multiplier=0,
                           allow_small_or_imprecise_dtypes=True).then_inc(made, 1)
            nc.gpsimd.iota(batch_row[:, :], pattern=[[S, NB]], base=0, channel_multiplier=0,
                           allow_small_or_imprecise_dtypes=True).then_inc(made, 1)

            def inverse_root(b, r):
                pool.wait_ge(ln_step[r], START + b * LN[r] + (2 * HALVES + 1))
                nc.gpsimd.tensor_tensor(rstd[:, r, :], veps[:, r, :], neg_half, ALU.pow).then_inc(rstd_ready[r], 1)

            inverse_root(0, 0)
            with pool.Fori(0, NB - 1) as b:
                inverse_root(b + 1, 0)
                inverse_root(b, 1)
            inverse_root(NB - 1, 1)

            pool.wait_ge(kv_stored, START + 16 * NB)
            pool.wait_ge(slots_zeroed, 16 * NB)

            def scatter_tile(b, h):
                if h == 0:
                    wait_alone(pool, "pool", staged, b * 32 + 32)
                for k in range(2):
                    pool.indirect_dma_start(
                        out=slot_dram, out_offset=bass.IndirectOffsetOnAxis(ap=istage[:, 2 * h + k:2 * h + k + 1], axis=0),
                        in_=xstage[:, h, :], in_offset=None, bounds_check=SLOTS - 1, oob_is_err=False).then_inc(scattered, 16)

            def gather_tile(t, h, first):
                wait_alone(pool, "pool", sim_copied, t + 1)
                nc.gpsimd.affine_select(out=z0, in_=z0, compare_op=ALU.not_equal, fill=0.0, base=P * h,
                                        pattern=[[-1, S]], channel_multiplier=1).then_inc(diag_cleared, 1)
                if not first:
                    wait_alone(pool, "pool", attn_step, (t - 1) * AS)
                for r in range(TOPK):
                    if r % 8 == 0:
                        wait_alone(pool, "pool", idx_ready, t * ROUNDS + (r // 8 + 1))
                    pool.indirect_dma_start(
                        out=kvg[:, h, r, :], out_offset=None, in_=kv_dram,
                        in_offset=bass.IndirectOffsetOnAxis(ap=gidx[:, h, r:r + 1], axis=0)).then_inc(gathered, 16)
                pool.wait_ge(gathered, (t + 1) * (16 * TOPK))
                if not (first and h == 0):
                    pool.wait_ge(attn_step, (t - 1) * AS + 1)
                nc.gpsimd.tensor_tensor(prod, kvg[:, h, :, 0:KD],
                                        qao[:, ds(t, 1), :].to_broadcast([P, TOPK, KD]), ALU.mult)\
                    .then_inc(prod_ready, 1)

            for h in range(HALVES):
                scatter_tile(0, h)
            for h in range(HALVES):
                gather_tile(h, h, True)
            with pool.Fori(1, NB) as b:
                for h in range(HALVES):
                    scatter_tile(b, h)
                for h in range(HALVES):
                    gather_tile(b * HALVES + h, h, False)

            def split(parts, high_done, low_done, before):
                for i, (w, high, low) in enumerate(parts):
                    nc.gpsimd.tensor_copy(high, w).then_inc(high_done, 1)
                    wait_alone(pool, "pool", high_done, before + (i + 1))
                    nc.gpsimd.tensor_tensor(low, w, high.bitcast(f32), ALU.subtract).then_inc(low_done, 1)
                    wait_alone(pool, "pool", low_done, before + (i + 1))

            with pool.Fori(2, E // 2) as j:
                for i in range(2):
                    wait_alone(pool, "pool", we_loaded, (j * 2 + (i + 1)) * 48)
                    wait_alone(pool, "pool", down_done, (j - 1) * GB + GPE * (i + 1))
                    split(expert_weights(i), we_high, we_low, j * 6 + 3 * i)
                    pool.wait_ge(attn_step, AS * NT)
                    pool.wait_ge(shared_loaded, 16 * 4)
                    if i == 0:
                        c = ds(j - 2, 1)
                        split([(swug[:, c, :], swug_r[0][:, c, :], swug_r[1][:, c, :])], shared_high, shared_split, (j - 2) * 2)
                    else:
                        c = ds((j - 2) * ((JC + 1) // 2), (JC + 1) // 2)
                        split([(swdn[:, c, :], swdn_r[0][:, c, :], swdn_r[1][:, c, :])], shared_high, shared_split, (j - 2) * 2 + 1)

            with pool.Fori(0, NCH) as c:
                pool.wait_ge(sgu_done, START + c * (JC + 1))
                nc.gpsimd.tensor_copy(xT_r[0][:, :, :], xT1[:, :, ds(c * (CT * P), CT * P)]).then_inc(xT_split, 1)
                wait_alone(pool, "pool", xT_split, c * 2 + 1)
                nc.gpsimd.tensor_tensor(xT_r[1][:, :, :], xT1[:, :, ds(c * (CT * P), CT * P)], xT_r[0][:, :, :].bitcast(f32),
                                        ALU.subtract).then_inc(xT_split, 1)
                pool.wait_ge(down_done, GB * (E // 2))
                pool.wait_ge(y_stored[0], 16 * GB // 2 * (E // 2))
                pool.wait_ge(y_stored[1], 16 * GB // 2 * (E // 2))
                pool.wait_ge(comb_step, START + c * CS)
                pool.wait_ge(aoT_done, START + c)
                nc.gpsimd.tensor_copy(aos, qao[:, ds(c * CT, CT), :]).then_inc(ao_fetched, 1)
                nc.gpsimd.tensor_copy(ysidx[:, :, :], slot_get[:, ds(c * CT, CT), :]).then_inc(ysidx_ready, 1)
                wait_alone(pool, "pool", ysidx_ready, c + 1)
                for n in range(CT):
                    for k in range(2):
                        pool.indirect_dma_start(
                            out=ys[:, n, k, :], out_offset=None, in_=yslot_dram,
                            in_offset=bass.IndirectOffsetOnAxis(ap=ysidx[:, n, k:k + 1], axis=0)).then_inc(ys_gathered, 16)
                pool.wait_ge(resid_loaded, c * 16 + 16)
                nc.gpsimd.tensor_tensor(resid, resid, xn1[:, ds(c * CT, CT), :], ALU.add).then_inc(resid_ready, 1)
                pool.wait_ge(resid_ready, c * 2 + 1)
                nc.gpsimd.tensor_tensor(resid, resid, bout[:, :].unsqueeze(1).to_broadcast([P, CT, D]), ALU.add)\
                    .then_inc(resid_ready, 1)

        @block.tensor
        def _(pe):
            pe.wait_ge(consts_loaded, CONSTS)
            pe.wait_ge(made, 10)

            def transpose_first(b):
                pe.wait_ge(ln_step[0], START + b * LN[0] + (LN[0] - 1))
                pe.wait_ge(xT1_kept, START + b)
                for h in range(HALVES):
                    for c in range(DC):
                        last = nc.tensor.transpose(ps_t1[:, c, h * P:(h + 1) * P], xn1s[:, h, c * P:(c + 1) * P], ident[:, :])
                last.then_inc(t1_ready, 1)

            def router_logits(b):
                pe.wait_ge(xT1s_ready, START + b + 1)
                pe.wait_ge(logits_saved, START + b)
                for h in range(HALVES):
                    for c in range(DC):
                        last = nc.tensor.matmul(ps_logit[:, h, :], xT1s[:, c, h * P:(h + 1) * P], router[:, c, :],
                                                start=(c == 0), stop=(c == DC - 1))
                last.then_inc(logits_ready, 1)

            def transpose_second(b):
                pe.wait_ge(ln_step[1], START + b * LN[1] + LN[1])
                pe.wait_ge(xn2T_ready, START + b * DC)
                for h in range(HALVES):
                    for c in range(DC):
                        last = nc.tensor.transpose(ps_t2[:, c, h * P:(h + 1) * P], xn2s[:, h, c * P:(c + 1) * P], ident[:, :])
                last.then_inc(t2_ready, 1)

            def project(b):
                pe.wait_ge(xn2T_ready, START + b * DC + DC)
                pe.wait_ge(h_saved, START + b * 2)
                for c in range(DC):
                    last = nc.tensor.matmul(ps_h, w1t[:, c, :], xn2T[:, c, :], start=(c == 0), stop=(c == DC - 1))
                last.then_inc(h_ready, 1)
                pe.wait_ge(qkv_saved, START + b * 2)
                for h in range(HALVES):
                    for c in range(DC):
                        last = nc.tensor.matmul(ps_qkv[:, h, 0:3 * KD], xn2T[:, c, h * P:(h + 1) * P], wqkvt[:, c, :],
                                                start=(c == 0), stop=(c == DC - 1))
                last.then_inc(qkv_ready, 1)

            transpose_first(0)
            router_logits(0)
            with pe.Fori(0, NB - 1) as b:
                transpose_first(b + 1)
                transpose_second(b)
                router_logits(b + 1)
                project(b)
            transpose_second(NB - 1)
            project(NB - 1)

            pe.wait_ge(h_saved, START + 2 * NB)
            pe.wait_ge(qkv_saved, START + 2 * NB)

            def count_choices():
                pe.wait_ge(hot_ready, 1)
                hv = hots.rearrange("p t e -> p (t e)")
                nc.tensor.matmul(ps[:, 7, 0:NT * E], earlier[:, :], hv, start=True, stop=True)
                nc.tensor.matmul(ps[:, 7, NT * E:2 * NT * E], ones[:, :], hv, start=True, stop=True).then_inc(counts_ready, 1)

            def layer2(b, s, first):
                pe.wait_ge(r1_dve, b * BSTEPS + (s + 1))
                pe.wait_ge(r1_act, b * BSTEPS + (s + 1))
                if not (first and s < PS2):
                    pe.wait_ge(r2_done, b * BSTEPS + (ps2_before(s) + 1))
                for u in range(2):
                    for v in range(2):
                        last = nc.tensor.matmul(ps_l2(s)[v * G2:(v + 1) * G2, u, :], w2t[:, :],
                                                r1[:, s % R1, 4 * u + 2 * v:4 * u + 2 * v + 2, :], start=True, stop=True)
                last.then_inc(l2_done, 1)

            def layer3(steps, s):
                pe.wait_ge(r2_done, steps)
                q, h = s % STEPS // 2, s // STEPS
                for a in range(2):
                    for c in range(4):
                        at = 32 - (UNIT * q + a)
                        last = nc.tensor.matmul(ps_sim(h)[32 * c:32 * c + 32, :], w3win[:, at:at + 32],
                                                r2[:, (s - 1 + c // 2) % R2, 512 * (c % 2) + a * S:512 * (c % 2) + (a + 1) * S],
                                                start=(q == 0 and a == 0), stop=(q == GROUPS - 1 and a == 1))
                last.then_inc(l3_done, 1)

            def pair_batch(b, first):
                for s in range(BSTEPS):
                    layer2(b, s, first)
                    if first and s == 12:
                        count_choices()
                    if first and s == STEPS:
                        pe.wait_ge(route_done, 1)
                    if s == 1 and not first:
                        layer3(b * BSTEPS, BSTEPS - 1)
                    elif s % 2 == 1 and s > 1:
                        if s % STEPS == 3 and not first:
                            pe.wait_ge(sim_copied, b * HALVES + (s // STEPS - 1))
                        layer3(b * BSTEPS + (s - 1), s - 2)

            pair_batch(0, True)
            with pe.Fori(1, NB) as b:
                pair_batch(b, False)
            layer3(NB * BSTEPS, BSTEPS - 1)

            def products(to, weights, moving, first, last_one):
                for i, (a, b) in enumerate(((0, 0), (0, 1), (1, 0))):
                    mm = nc.tensor.matmul(to, weights[a], moving[b], start=(first and i == 0), stop=(last_one and i == 2))
                return mm

            def transpose_slots(j, g, first):
                if first and g < 2:
                    pe.wait_ge(sim_copied, NT - 1 + g)
                else:
                    pe.wait_ge(xt_low, j * GB + (g - 1))
                pe.wait_ge(xe_loaded[g % GPE], j * 32 + (g // GPE + 1) * 16)
                for n in range(2):
                    for c in range(DC):
                        last = nc.tensor.transpose(ps_xt(g)[:, c, n * P:(n + 1) * P],
                                                   xe[g % GPE][:, n, c * P:(c + 1) * P], ident[:, :])
                last.then_inc(xt_done, 1)

            def gate_up(j, g, first):
                i = g // GPE
                if g % GPE == 0:
                    pe.wait_ge(we_low, j * 6 + (3 * i + 3))
                pe.wait_ge(xt_low, j * GB + (g + 1))
                if not (first and g < 2):
                    pe.wait_ge(mul_done, j * GB + (g - 1))
                for to, col, w in ((ps_gate(g), 0, IM), (ps_up(g), IM, IM), (ps_tail(g), 2 * IM, 2 * TAIL)):
                    for c in range(DC):
                        last = products(to, [h[:, c, col:col + w] for h in wug_r[i]], [h[:, c, :] for h in xTe_r[g % 2]],
                                        c == 0, c == DC - 1)
                last.then_inc(gu_done, 1)

            def down(j, g, first):
                pe.wait_ge(h_low, j * GB + (g + 1))
                if not (first and g < 2):
                    pe.wait_ge(down_copied, j * GB + (g - 1))
                i = (g // GPE) % 2
                for n in range(2):
                    for m, rows in enumerate((slice(0, IM), slice(TAIL, 2 * TAIL))):
                        last = products(ps_down(g)[:, n, :], [h[rows, m, n * P:(n + 1) * P] for h in hTe_r[g % 2]],
                                        [h[rows, m, :] for h in wdn_r[i]], m == 0, m == 1)
                last.then_inc(down_done, 1)

            def expert_pair(j, first):
                transpose_slots(j, 0, first)
                for g in range(GB):
                    if g < GB - 1:
                        transpose_slots(j, g + 1, first)
                    gate_up(j, g, first)
                    if not (first and g == 0):
                        down(j, g - 1, first)

            expert_pair(0, True)
            with pe.Fori(1, E // 2) as j:
                expert_pair(j, False)
            down(E // 2 - 1, GB - 1, False)

            pe.wait_ge(shared_split, 4)
            pe.wait_ge(down_copied, GB * (E // 2))

            with pe.Fori(0, NCH) as c:
                pe.wait_ge(xT_split, c * 2 + 2)
                for m in range(JC + 1):
                    if m == JC:
                        pe.wait_ge(ao_fetched, c + 1)
                        wait_alone(pe, "pe", aoT_low, START + c)
                        for n in range(CT):
                            last = nc.tensor.transpose(ps[0:KD, 4, n * P:(n + 1) * P], aos[:, n, :], ident[:, :])
                        last.then_inc(aoT_done, 1)
                    if 2 <= m < JC:
                        pe.wait_ge(smul_done, c * (JC + 1) + (m - 1))
                    for bank, at in ((2 * (m % 2), m * P), (2 * (m % 2) + 1, (JC + m) * P)) if m < JC else ((5, 2 * JC * P),):
                        for k in range(DC):
                            last = products(ps[:, bank, :], [w[:, k, at:at + P] for w in swug_r], [x[:, k, :] for x in xT_r],
                                            k == 0, k == DC - 1)
                    last.then_inc(sgu_done, 1)

                def down(n, ms):
                    for m in ms:
                        last = products(ps[:, 6 + n // 2, (n % 2) * D:(n % 2 + 1) * D], [h[:, m, n * P:(n + 1) * P] for h in hTs_r],
                                        [w[:, m, :] for w in swdn_r], m == 0, m == JC)
                    if m == JC:
                        last.then_inc(sdown_done, 1)

                pe.wait_ge(comb_step, START + c * CS)
                pe.wait_ge(slow_done, c * (JC + 1) + (JC - 1))
                for n in (0, 2):
                    down(n, range(JC - 1))
                pe.wait_ge(slow_done, c * (JC + 1) + JC)
                for n in (0, 2):
                    down(n, (JC - 1,))
                pe.wait_ge(slow_done, (c + 1) * (JC + 1))
                pe.wait_ge(aoT_low, START + c + 1)
                for n in (0, 2):
                    down(n, (JC,))
                for n in (1, 3):
                    down(n, range(JC + 1))

        def step_rows(s):
            return [32 * (2 * (s % 2) + k // UNIT) + UNIT * (s % STEPS // 2) + k % UNIT for k in range(STEP_ROWS)]

        @block.scalar
        def _(act):
            act.wait_ge(consts_loaded, CONSTS)

            def keep_first(b):
                act.wait_ge(ln_step[0], START + b * LN[0] + (LN[0] - 1))
                nc.scalar.activation(xn1[:, ds(b * HALVES, HALVES), :], xn1s, ACT.Copy).then_inc(ln_step[0], 1)
                act.wait_ge(t1_ready, START + b + 1)
                act.wait_ge(logits_ready, START + b)
                nc.scalar.activation(xT1s, ps_t1, ACT.Copy).then_inc(xT1s_ready, 1)
                nc.scalar.activation(xT1[:, :, ds(b * S, S)], ps_t1, ACT.Copy).then_inc(xT1_kept, 1)

            def keep_second(b):
                act.wait_ge(t2_ready, START + b + 1)
                act.wait_ge(qkv_ready, START + b)
                for c in range(DC):
                    nc.scalar.activation(xn2T[:, c, :], ps_t2[:, c, :], ACT.Identity, scale=gamma[:, c:c + 1],
                                         bias=beta[:, c:c + 1]).then_inc(xn2T_ready, 1)
                act.wait_ge(h_ready, b + 1)
                nc.scalar.activation(hneg[:, ds(b * S, S)], ps_h, ACT.Copy, scale=-1.0).then_inc(h_saved, 1)
                nc.scalar.activation(hb[:, ds(b * S, S)], ps_h, ACT.Identity, bias=b1[:, 0:1]).then_inc(h_saved, 1)

            keep_first(0)
            with act.Fori(0, NB - 1) as b:
                keep_first(b + 1)
                keep_second(b)
            keep_second(NB - 1)
            act.wait_ge(qkv_ready, START + NB)
            act.wait_ge(h_saved, START + 2 * NB)
            act.wait_ge(xT1_kept, START + NB)

            def relu1(b, s, first):
                if not (first and s < R1):
                    act.wait_ge(l2_done, b * BSTEPS + (s - R1 + 1))
                rows = step_rows(s)
                for k in range(dve_rows(s), STEP_ROWS):
                    at = b * S + ((s // STEPS) * P + rows[k])
                    last = nc.scalar.activation(r1[:, s % R1, k, :], hneg[:, ds(b * S, S)], ACT.Relu, bias=hb[:, ds(at, 1)])
                last.then_inc(r1_act, 1)

            def relu2(steps, s, wait_group):
                act.wait_ge(l2_done, steps)
                if wait_group is None and s == 0:
                    act.wait_ge(slots_zeroed, 16 * NB)
                    act.wait_ge(kv_stored, START + 16 * NB)
                if wait_group is not None:
                    act.wait_ge(l3_done, wait_group)
                nc.scalar.activation(r2[:, s % R2, :].rearrange("p (u n) -> p u n", u=2), ps_l2(s), ACT.Relu, bias=b2[:, 0:1]).then_inc(r2_done, 1)

            def copy_sim(t, h, first):
                act.wait_ge(l3_done, t * GROUPS + GROUPS)
                if not first:
                    act.wait_ge(topk_step, t * TS)
                nc.scalar.activation(z0, ps_sim(h), ACT.Identity, bias=b3[:, 0:1]).then_inc(sim_copied, 1)

            def exp_scores(t):
                act.wait_ge(attn_step, t * AS + 3)
                nc.scalar.activation(sc, sc, ACT.Exp, scale=SCALE).then_inc(exp_ready, 1)

            def pair_batch(b, first):
                for s in range(BSTEPS):
                    h = s // STEPS
                    relu1(b, s, first)
                    if first and s == 9:
                        act.wait_ge(dlog_ready, 1)
                        nc.scalar.activation(edlog, dlog, ACT.Exp).then_inc(exp_routed, 1)
                    if s % STEPS == 3 and not (first and h == 0):
                        copy_sim(b * HALVES + (h - 1), 1 - h, first)
                    if not (first and s == 0):
                        relu2(b * BSTEPS + s, (s - 1) % BSTEPS, None if first and s - 1 < R2 else b * (BSTEPS // 2) + ((s - 1) // 2 - 1))
                    if s % STEPS == 10 and not first:
                        exp_scores(b * HALVES + (h - 2))

            pair_batch(0, True)
            with act.Fori(1, NB) as b:
                pair_batch(b, False)
            relu2(NB * BSTEPS, BSTEPS - 1, NB * (BSTEPS // 2) - 2)

            act.wait_ge(r1_dve, NB * BSTEPS)

            def weights_high(e):
                act.wait_ge(we_loaded, (e + 1) * 48)
                if e >= 2:
                    act.wait_ge(down_done, (e - 1) * GPE)
                for w, high, low in expert_weights(e % 2):
                    nc.scalar.activation(high, w, ACT.Copy).then_inc(we_high, 1)

            def slots_high(j, g, first):
                act.wait_ge(xt_done, j * GB + (g + 1))
                if not (first and g < 2):
                    act.wait_ge(gu_done, j * GB + (g - 1))
                nc.scalar.activation(xTe_r[g % 2][0][:, :, :], ps_xt(g), ACT.Copy).then_inc(xt_high, 1)

            def copy_down(j, g, first):
                act.wait_ge(down_done, j * GB + (g + 1))
                if not (first and g < 2):
                    act.wait_ge(y_stored[g % 2], j * (GB // 2 * 16) + g // 2 * 16)
                nc.scalar.activation(oute[g % 2], ps_down(g), ACT.Copy).then_inc(down_copied, 1)

            def expert_pair(j, peeled):
                first = peeled and j == 0
                if not first:
                    slots_high(j, 0, first)
                for g in range(GB):
                    if g < GB - 1 and not (first and g == 0):
                        slots_high(j, g + 1, first)
                    act.wait_ge(gu_done, j * GB + (g + 1))
                    if not (first and g < 2):
                        act.wait_ge(h_low, j * GB + (g - 1))
                    nc.scalar.activation(sge[g % 2][0:IM, 0, :], ps_gate(g), ACT.Silu)
                    nc.scalar.activation(sge[g % 2][TAIL:2 * TAIL, 1, :], ps_tail(g)[0:TAIL], ACT.Silu).then_inc(silu_done, 1)
                    act.wait_ge(mul_done, j * GB + (g + 1))
                    if not (first and g < 2):
                        act.wait_ge(down_done, j * GB + (g - 1))
                    for rows, h, high, low in expert_activations(g):
                        last = nc.scalar.activation(high, h, ACT.Copy)
                    last.then_inc(h_high, 1)
                    if not (first and g == 0):
                        copy_down(j, g - 1, first)
                    if peeled and (j, g) in WEIGHTS_AT:
                        weights_high(WEIGHTS_AT[j, g])
                    if peeled and j == 1 and g == 5:
                        exp_scores(NT - 1)

            weights_high(0)
            copy_sim(NT - 1, 1, False)
            for g in range(2):
                slots_high(0, g, True)
            exp_scores(NT - 2)
            for j in range(2):
                expert_pair(j, True)
            with act.Fori(2, E // 2) as j:
                expert_pair(j, False)
            copy_down(E // 2 - 1, GB - 1, False)
            act.wait_ge(down_done, GB * (E // 2))

            with act.Fori(0, NCH) as c:
                def high(m):
                    rows = slice(0, P) if m < JC else slice(KD, KD + TAIL)
                    act.wait_ge(smul_done, c * (JC + 1) + (m + 1))
                    nc.scalar.activation(hTs_r[0][rows, m, :], sgs[m % 2][rows], ACT.Copy).then_inc(shigh_done, 1)

                act.wait_ge(sdown_done, START + c * CT)
                for m in range(JC + 1):
                    if m == JC:
                        act.wait_ge(aoT_done, START + c + 1)
                        nc.scalar.activation(hTs_r[0][0:KD, JC, :], ps[0:KD, 4, :], ACT.Copy).then_inc(aoT_high, 1)
                    act.wait_ge(sgu_done, START + c * (JC + 1) + (m + 1))
                    if m >= 2:
                        act.wait_ge(slow_done, c * (JC + 1) + (m - 1))
                    if m < JC:
                        nc.scalar.activation(sgs[m % 2], ps[:, 2 * (m % 2), :], ACT.Silu).then_inc(ssilu_done, 1)
                    else:
                        nc.scalar.activation(sgs[m % 2][KD:KD + TAIL], ps[0:TAIL, 5, :], ACT.Silu).then_inc(ssilu_done, 1)
                    if m:
                        high(m - 1)
                high(JC)

        @block.vector
        def _(dve):
            def tokens(b, h):
                return xn1[:, ds(b * HALVES + h, 1), :].rearrange("p o d -> p (o d)")

            def statistics(*which):
                for b, r in which:
                    dve.wait_ge(ln_step[r], START + b * LN[r])
                    if r:
                        dve.wait_ge(ln_step[0], START + (b + 1) * LN[0])
                    for h in range(HALVES):
                        nc.vector.bn_stats(stats[:, r, h, :], tokens(b, h)).then_inc(ln_step[r], 1)
                for h in range(HALVES):
                    for b, r in which:
                        wait_alone(dve, "dve", ln_step[r], START + b * LN[r] + (HALVES + h))
                        nc.vector.bn_aggr(mv[:, r, h, :], stats[:, r, h, :]).then_inc(ln_step[r], 1)
                for b, r in which:
                    dve.wait_ge(ln_step[r], START + b * LN[r] + 2 * HALVES)
                    nc.vector.tensor_scalar(veps[:, r, :], mv[:, r, :, 1], EPS, None, ALU.add).then_inc(ln_step[r], 1)

            def normalize(b, r):
                dve.wait_ge(rstd_ready[r], b + 1)
                dve.wait_ge(t2_ready if r else t1_ready, START + b)
                for h in range(HALVES):
                    nc.vector.tensor_scalar((xn2s if r else xn1s)[:, h, :], tokens(b, h), mv[:, r, h, 0:1],
                                            rstd[:, r, h:h + 1], ALU.subtract, ALU.mult).then_inc(ln_step[r], 1)

            def save_logits(b):
                dve.wait_ge(logits_ready, START + b + 1)
                nc.vector.tensor_copy(logits[:, ds(b * HALVES, HALVES), :], ps_logit).then_inc(logits_saved, 1)

            def save_projections(b):
                dve.wait_ge(qkv_ready, START + b + 1)
                nc.vector.tensor_tensor(qao[:, ds(b * HALVES, HALVES), :], ps_qkv[:, :, 0:KD],
                                        bqkv[:, 0:KD].unsqueeze(1).to_broadcast([P, HALVES, KD]), ALU.add).then_inc(qkv_saved, 1)
                dve.wait_ge(kv_stored, START + b * 16)
                nc.vector.tensor_tensor(kvs, ps_qkv[:, :, KD:3 * KD],
                                        bqkv[:, KD:3 * KD].unsqueeze(1).to_broadcast([P, HALVES, 2 * KD]), ALU.add)\
                    .then_inc(qkv_saved, 1)

            dve.wait_ge(x_loaded, 16)
            statistics((0, 0))
            normalize(0, 0)

            def both_layernorms(b):
                dve.wait_ge(x_loaded, b * 16 + 32)
                statistics((b + 1, 0), (b, 1))
                normalize(b + 1, 0)
                normalize(b, 1)
                save_logits(b)

            both_layernorms(0)
            dve.wait_ge(consts_loaded, CONSTS)
            with dve.Fori(1, NB - 1) as b:
                both_layernorms(b)
                save_projections(b - 1)
            statistics((NB - 1, 1))
            normalize(NB - 1, 1)
            save_logits(NB - 1)
            save_projections(NB - 2)
            save_projections(NB - 1)

            steps = [0]

            def link(ins):
                steps[0] += 1
                ins.then_inc(route_step, 1)
                dve.wait_ge(route_step, steps[0])

            ROUTED = NT // 4

            def route(s):
                if 2 <= s < 6:
                    for t in range((s - 2) * ROUTED, (s - 1) * ROUTED):
                        nc.vector.max(best[:, t, :], logits[:, t, :]).then_inc(route_step, 1)
                        steps[0] += 1
                if s == 6:
                    dve.wait_ge(route_step, steps[0])
                    link(nc.vector.tensor_tensor(dlog.rearrange("p (t o) -> p t o", o=1), best[:, :, 1:2], best[:, :, 0:1], ALU.subtract))
                    dve.sem_inc(dlog_ready, 1)
                if 6 <= s < 10:
                    for t in range((s - 6) * ROUTED, (s - 5) * ROUTED):
                        nc.vector.max_index(besti[:, t, :], best[:, t, :], logits[:, t, :]).then_inc(route_step, 1)
                        steps[0] += 1
                if s == 10:
                    dve.wait_ge(route_step, steps[0])
                    link(nc.vector.tensor_copy(expert, besti[:, :, 0:2]))
                    for k in range(2):
                        link(nc.vector.tensor_tensor(hot[k], iota8[:, :].unsqueeze(1).to_broadcast([P, NT, E]),
                                                     expert[:, :, k:k + 1].to_broadcast([P, NT, E]), ALU.is_equal))
                    nc.vector.tensor_tensor(hots, hot[0], hot[1], ALU.add).then_inc(hot_ready, 1)
                w0 = route_w[:, :, 0:1].rearrange("p t o -> p (t o)")
                w1 = route_w[:, :, 1:2].rearrange("p t o -> p (t o)")
                if s == 11:
                    dve.wait_ge(exp_routed, 1)
                    link(nc.vector.tensor_scalar(eden, edlog, 1.0, None, ALU.add))
                    link(nc.vector.reciprocal(w0, eden))
                    link(nc.vector.tensor_tensor(w1, w0, edlog, ALU.mult))
                if s == 13:
                    dve.wait_ge(counts_ready, 1)
                    for e in range(E):
                        link(nc.vector.tensor_tensor_scan(filled[:, :, e], ones[:, 0:NT], ps_count[:, :, e], 0.0, ALU.mult, ALU.add))
                if s == 14:
                    link(nc.vector.tensor_tensor(base, filled, ps_count, ALU.subtract))
                    link(nc.vector.tensor_tensor(base, base, ps_before, ALU.add))
                    for k in range(2):
                        link(nc.vector.tensor_tensor(hotpos[k], hot[k], base, ALU.mult))
                        link(nc.vector.tensor_reduce(pos[:, :, k], hotpos[k], AX, ALU.add))
                if s == 15:
                    link(nc.vector.tensor_scalar(posc, pos, float(CAP - 1), None, ALU.min))
                    link(nc.vector.tensor_scalar(valid, pos, float(CAP), None, ALU.is_lt))
                    link(nc.vector.tensor_scalar(over, pos, float(CAP), float(2 * SLOTS), ALU.is_ge, ALU.mult))
                    link(nc.vector.scalar_tensor_tensor(slotf, expert, float(CAP), posc, ALU.mult, ALU.add))
                    link(nc.vector.tensor_copy(slot_get[:, :, :], slotf))
                    link(nc.vector.tensor_tensor(slot_put[:, :].rearrange("p (t k) -> p t k", k=2), slotf, over, ALU.add))
                    link(nc.vector.tensor_tensor(route_w[:, :, :], route_w[:, :, :], valid, ALU.mult))
                    dve.sem_inc(route_done, 1)

            dve.wait_ge(made, 10)
            dve.wait_ge(qkv_saved, START + 2 * NB)
            dve.wait_ge(logits_saved, START + NB)
            dve.wait_ge(h_saved, START + 2 * NB)
            dve.wait_ge(xT1_kept, START + NB)

            def relu1_begin(b, s, first):
                if not (first and s < R1):
                    dve.wait_ge(l2_done, b * BSTEPS + (s - R1 + 1))

            def relu1_rows(b, s, ks):
                rows = step_rows(s)
                for k in ks:
                    at = b * S + ((s // STEPS) * P + rows[k])
                    row = nc.vector.tensor_scalar(r1[:, s % R1, k, :], hneg[:, ds(b * S, S)], hb[:, ds(at, 1)], 0.0, ALU.add, ALU.max)
                    if k == dve_rows(s) - 1:
                        row.then_inc(r1_dve, 1)

            zs = [z0, z1, z0, z1]


            def topk_max(t, r):
                if r == 0:
                    wait_alone(dve, "dve", diag_cleared, t + 1)
                else:
                    wait_alone(dve, "dve", topk_step, t * TS + 3 * r)
                nc.vector.max(top8[:, r, :], zs[r]).then_inc(topk_step, 1)

            def topk_find(t, r):
                wait_alone(dve, "dve", topk_step, t * TS + (3 * r + 1))
                if r < ROUNDS - 1:
                    nc.vector.match_replace(zs[r + 1], top8[:, r, :], zs[r], LOWEST).then_inc(topk_step, 1)
                nc.vector.max_index(idx8[:, r, :], top8[:, r, :], zs[r]).then_inc(topk_step, 1)

            def topk_rows(t, h, b, r):
                dve.wait_ge(topk_step, t * TS + min(3 * r + 3, TS))
                nc.vector.tensor_scalar(gidx[:, h, 8 * r:8 * r + 8], idx8[:, r, :], batch_row[:, ds(b, 1)], None, ALU.add)\
                    .then_inc(idx_ready, 1)

            def attention(t, h, a):
                n = t * AS
                if a == 0:
                    dve.wait_ge(prod_ready, t + 1)
                    nc.vector.tensor_tensor(sc.rearrange("p r h -> p (r h)"),
                                            prod.rearrange("p r (h d) -> p (r h) d", d=2)[:, :, 0],
                                            prod.rearrange("p r (h d) -> p (r h) d", d=2)[:, :, 1], ALU.add).then_inc(attn_step, 1)
                elif a == 1:
                    dve.wait_ge(attn_step, n + 1)
                    nc.vector.tensor_reduce(smax[:, :], sc.rearrange("p r h -> p h r"), AX, ALU.max).then_inc(attn_step, 1)
                elif a == 2:
                    dve.wait_ge(attn_step, n + 2)
                    nc.vector.tensor_tensor(sc, sc, smax[:, :].unsqueeze(1).to_broadcast([P, TOPK, HEADS]), ALU.subtract)\
                        .then_inc(attn_step, 1)
                elif a == 3:
                    dve.wait_ge(exp_ready, t + 1)
                    nc.vector.tensor_reduce(sden[:, :], sc.rearrange("p r h -> p h r"), AX, ALU.add).then_inc(attn_step, 1)
                elif a == 4:
                    dve.wait_ge(attn_step, n + 4)
                    nc.vector.reciprocal(srec[:, :], sden[:, :]).then_inc(attn_step, 1)
                elif a == 5:
                    nc.vector.tensor_tensor(pv.rearrange("p r (h d) -> p r h d", d=2),
                                            kvg[:, h, :, KD:2 * KD].rearrange("p r (h d) -> p r h d", d=2),
                                            sc.unsqueeze(3).to_broadcast([P, TOPK, HEADS, 2]), ALU.mult).then_inc(attn_step, 1)
                elif a == 6:
                    dve.wait_ge(attn_step, n + 6)
                    nc.vector.tensor_reduce(aosum[:, :], pv.rearrange("p r k -> p k r"), AX, ALU.add).then_inc(attn_step, 1)
                elif a == 7:
                    dve.wait_ge(attn_step, n + 7)
                    nc.vector.tensor_tensor(qao[:, ds(t, 1), :].rearrange("p o (h d) -> p (o h) d", d=2),
                                            aosum[:, :].rearrange("p (h d) -> p h d", d=2),
                                            srec[:, :].unsqueeze(2).to_broadcast([P, HEADS, 2]), ALU.mult).then_inc(attn_step, 1)

            AT = {7: (0,), 8: (1,), 9: (2,), 13: (3,), 14: (4, 5), 15: (6, 7)}
            TOP = 6

            def pair_batch(b, first):
                for s in range(BSTEPS):
                    h, s16 = s // STEPS, s % STEPS
                    r = s16 - TOP
                    topk = 0 <= r <= ROUNDS and not (first and h == 0)
                    prev, prev_b = b * HALVES + (h - 1), b if h else b - 1
                    n = dve_rows(s)
                    if first and s < STEPS:
                        route(s)
                    relu1_begin(b, s, first)
                    relu1_rows(b, s, range(2))
                    if topk and r < ROUNDS:
                        topk_max(prev, r)
                    if topk and r:
                        topk_rows(prev, 1 - h, prev_b, r - 1)
                    for a in () if first else AT.get(s16, ()):
                        attention(b * HALVES + (h - 2), h, a)
                    relu1_rows(b, s, range(2, n))
                    if topk and r < ROUNDS:
                        topk_find(prev, r)

            pair_batch(0, True)
            with dve.Fori(1, NB) as b:
                pair_batch(b, False)

            def weights_low(e):
                for i, (w, high, low) in enumerate(expert_weights(e % 2)):
                    dve.wait_ge(we_high, 3 * e + (i + 1))
                    nc.vector.tensor_tensor(low, w, high.bitcast(f32), ALU.subtract).then_inc(we_low, 1)

            def slots_low(j, g):
                dve.wait_ge(xt_high, j * GB + (g + 1))
                nc.vector.tensor_tensor(xTe_r[g % 2][1][:, :, :], ps_xt(g), xTe_r[g % 2][0][:, :, :].bitcast(f32), ALU.subtract)\
                    .then_inc(xt_low, 1)

            def gate_times_up(j, g):
                dve.wait_ge(silu_done, j * GB + (g + 1))
                for (rows, h, high, low), up in zip(expert_activations(g), (ps_up(g), ps_tail(g)[TAIL:2 * TAIL])):
                    last = nc.vector.tensor_tensor(h, h, up, ALU.mult)
                last.then_inc(mul_done, 1)

            def activations_low(j, g):
                dve.wait_ge(h_high, j * GB + (g + 1))
                for rows, h, high, low in expert_activations(g):
                    last = nc.vector.tensor_tensor(low, h, high.bitcast(f32), ALU.subtract)
                last.then_inc(h_low, 1)

            EAT = [{4: (3, 4), 5: (5,), 6: (6,), 7: (7,)}, {2: (0,), 3: (1,), 4: (2,), 6: (3,), 7: (4, 5), 8: (6,), 9: (7,)}]

            def expert_pair(j, peeled):
                first = peeled and j == 0
                if not first:
                    slots_low(j, 0)
                for g in range(GB):
                    if g < GB - 1 and not (first and g == 0):
                        slots_low(j, g + 1)
                    gate_times_up(j, g)
                    activations_low(j, g)
                    if first and g < ROUNDS:
                        topk_max(NT - 1, g)
                        topk_find(NT - 1, g)
                        topk_rows(NT - 1, 1, NB - 1, g)
                    if peeled and (j, g) in WEIGHTS_AT:
                        weights_low(WEIGHTS_AT[j, g])
                    for a in EAT[j].get(g, ()) if peeled else ():
                        attention(NT - 2 + j, j, a)

            weights_low(0)
            for g in range(2):
                slots_low(0, g)
            for a in range(3):
                attention(NT - 2, 0, a)
            for j in range(2):
                expert_pair(j, True)
            with dve.Fori(2, E // 2) as j:
                expert_pair(j, False)

            with dve.Fori(0, NCH) as c:
                def low(m):
                    rows = slice(0, P) if m < JC else slice(KD, KD + TAIL)
                    dve.wait_ge(shigh_done, c * (JC + 1) + (m + 1))
                    nc.vector.tensor_tensor(hTs_r[1][rows, m, :], sgs[m % 2][rows], hTs_r[0][rows, m, :].bitcast(f32), ALU.subtract)\
                        .then_inc(slow_done, 1)

                dve.wait_ge(sdown_done, START + c * CT)
                for m in range(JC + 1):
                    if m == JC:
                        dve.wait_ge(aoT_high, c + 1)
                        nc.vector.tensor_tensor(hTs_r[1][0:KD, JC, :], ps[0:KD, 4, :], hTs_r[0][0:KD, JC, :].bitcast(f32), ALU.subtract)\
                            .then_inc(aoT_low, 1)
                    dve.wait_ge(ssilu_done, c * (JC + 1) + (m + 1))
                    rows, bank = (slice(0, P), 2 * (m % 2) + 1) if m < JC else (slice(KD, KD + TAIL), 5)
                    nc.vector.tensor_tensor(sgs[m % 2][rows], sgs[m % 2][rows], ps[rows, bank, :], ALU.mult)\
                        .then_inc(smul_done, 1)
                    if m:
                        low(m - 1)
                low(JC)
                dve.wait_ge(ys_gathered, c * (16 * 2 * CT) + 16 * 2 * CT)
                dve.wait_ge(out_stored, START + c * 16)
                for n in range(CT):
                    dve.wait_ge(sdown_done, START + c * CT + (n // 2 + 3))
                    nc.vector.scalar_tensor_tensor(fin[:, n, :], ys[:, n, 0, :], route_w[:, ds(c * CT + n, 1), 0:1].rearrange("p a b -> p (a b)"),
                                                   ps[:, 6 + n // 2, (n % 2) * D:(n % 2 + 1) * D], ALU.mult, ALU.add)\
                        .then_inc(comb_step, 1)
                for n in range(CT):
                    dve.wait_ge(comb_step, START + c * CS + (n + 1))
                    nc.vector.scalar_tensor_tensor(fin[:, n, :], ys[:, n, 1, :], route_w[:, ds(c * CT + n, 1), 1:2].rearrange("p a b -> p (a b)"),
                                                   fin[:, n, :], ALU.mult, ALU.add).then_inc(comb_step, 1)
                dve.wait_ge(resid_ready, c * 2 + 2)
                for n in range(CT):
                    dve.wait_ge(comb_step, START + c * CS + (CT + n + 1))
                    nc.vector.tensor_tensor(fin[:, n, :], fin[:, n, :], resid[:, n, :], ALU.add).then_inc(comb_step, 1)


_PRE = "L0_attn_"
_INS = [("L0_attn_x", False), ("L0_attn_gamma", False), ("L0_attn_beta", False), ("L0_attn_W1", True), ("L0_attn_b1", False),
        ("L0_attn_W2", True), ("L0_attn_b2", False), ("L0_attn_W3", False), ("L0_attn_b3", False), ("L0_attn_Wqkv", True),
        ("L0_attn_bqkv", False), ("L0_attn_Wout", True), ("L0_attn_bout", False), ("L0_ffn_router", False),
        ("L0_ffn_w_up_gate", False), ("L0_ffn_w_down", False), ("L0_ffn_shared_w_up_gate", False),
        ("L0_ffn_shared_w_down", False)]
_OUTS = [((16, 256, 256), "float32")]


def kernel(**inputs):
    import numpy as _np
    import concourse.bacc as _bacc
    from concourse import mybir as _mybir
    from concourse.bass_utils import run_bass_kernel_spmd as _run

    nc = _bacc.Bacc("TRN2", target_bir_lowering=False, num_devices=1)
    arrays, args = {}, []
    for name, transposed in _INS:
        a = _np.asarray(inputs[name])
        if transposed:
            a = a.T
        elif name.endswith("up_gate"):
            g = a.reshape(a.shape[:-1] + (2, a.shape[-1] // 2))
            main, tail = g[..., :-64], g[..., -64:]
            a = _np.concatenate([p.reshape(a.shape[:-1] + (-1,)) for p in (main, tail)], axis=-1)
        a = _np.ascontiguousarray(a)
        arrays[f"in_{name}_dram"] = a
        args.append(nc.dram_tensor(f"in_{name}_dram", a.shape, _mybir.dt.from_np(a.dtype), kind="ExternalInput").ap())
    for i, (shape, dtype) in enumerate(_OUTS):
        dt = _mybir.dt.from_np(_np.dtype(dtype))
        args.append(nc.dram_tensor(f"out_{i}_dram", shape, dt, kind="ExternalOutput").ap())
    lsn_attention_moe_block(nc, *args)
    r = _run(nc, [arrays], core_ids=[0])
    got = tuple(r.results[0][f"out_{i}_dram"] for i in range(len(_OUTS)))
    return got[0]
```
